# Optimizing a Trainium2 kernel written in Bass

```python
import numpy as np
import jax
import jax.numpy as jnp

def _softmax(x, axis=-1):
    return jax.nn.softmax(x, axis=axis)

def _gelu(x):
    return jax.nn.gelu(x, approximate=True)

def _silu(x):
    return jax.nn.silu(x)

def _sigmoid(x):
    return jax.nn.sigmoid(x)

def _layernorm(x, axis=-1, eps=1e-05):
    m = jnp.mean(x, axis=axis, keepdims=True)
    v = jnp.var(x, axis=axis, keepdims=True)
    return (x - m) / jnp.sqrt(v + eps)

def _scatter_add(tgt, idx, src, axis=0):
    return tgt.at[idx].add(src)

def _segment_sum(src, seg, n):
    return jax.ops.segment_sum(src, seg, n)
kernel_name = 'mk_adaln_ffn_d2_seqx_r4_85c54b'

def setup_inputs(seed: int=0):
    np.random.seed(seed)
    _w = jnp.asarray

    def _rec_inputs():
        import jax
        import jax.numpy as jnp
        _rk = jax.random.key(seed)
        x = -0.0003929 + 0.9999 * jax.random.normal(jax.random.fold_in(_rk, 1), (64, 64, 256), jnp.float32)
        _lenS = 64 - jax.random.randint(jax.random.fold_in(_rk, 7), (64,), 0, max(1, 64 // 4) + 1, jnp.int32)
        _lenS2 = 64 - jax.random.randint(jax.random.fold_in(_rk, 8), (64,), 0, max(1, 64 // 4) + 1, jnp.int32)
        itok_B_0_63 = jax.random.randint(jax.random.fold_in(_rk, 11), (64,), 0, 64, jnp.int32)
        itok_B_0_8 = jax.random.randint(jax.random.fold_in(_rk, 12), (64,), 0, 9, jnp.int32)
        return (x, itok_B_0_63, itok_B_0_8)
    x, itok_B_0_63, itok_B_0_8 = _rec_inputs()

    def _L0_cond_setup():
        import jax, jax.numpy as jnp
        import numpy as np
        NUM_CATEGORIES = 64
        INPUT_DIM = 256
        HIDDEN_DIM = 256
        B = 64
        S = 64
        key = jax.random.key(seed)
        kx, kc, kw = jax.random.split(key, 3)
        x = jax.random.normal(kx, (B, S, INPUT_DIM), dtype=jnp.float32)
        cat_ids = jax.random.randint(kc, (B,), 0, NUM_CATEGORIES, dtype=jnp.int32)
        W = 0.02 * jax.random.normal(kw, (NUM_CATEGORIES, INPUT_DIM, HIDDEN_DIM), dtype=jnp.float32)
        b = jnp.zeros((NUM_CATEGORIES, HIDDEN_DIM), dtype=jnp.float32)
        return {'x': x, 'cat_ids': cat_ids, 'W': W, 'b': b}
    _L0_cond_all = _L0_cond_setup()
    _L0_cond_in = {k: v for k, v in _L0_cond_all.items() if k in ('W', 'b')}
    del _L0_cond_all

    def _L0_ffn_setup():
        import jax, jax.numpy as jnp
        import numpy as np
        D_MODEL = 256
        key = jax.random.key(seed)
        k_x, k_w, k_a1, k_a2 = jax.random.split(key, 4)
        x = jax.random.normal(k_x, (4, 512, D_MODEL), dtype=jnp.float32)
        weight = jax.random.normal(k_w, (D_MODEL, D_MODEL), dtype=jnp.float32) * 0.02
        aux_weight1 = jax.random.normal(k_a1, (D_MODEL, D_MODEL), dtype=jnp.float32) * 0.02
        aux_weight2 = jax.random.normal(k_a2, (D_MODEL, D_MODEL), dtype=jnp.float32) * 0.02
        bias = jnp.zeros((D_MODEL,), dtype=jnp.float32)
        return {'x': x, 'weight': weight, 'aux_weight1': aux_weight1, 'aux_weight2': aux_weight2, 'bias': bias}
    _L0_ffn_all = _L0_ffn_setup()
    _L0_ffn_in = {k: v for k, v in _L0_ffn_all.items() if k in ('weight', 'aux_weight1', 'aux_weight2', 'bias')}
    del _L0_ffn_all

    def _L1_cond_setup():
        import jax, jax.numpy as jnp
        import numpy as np
        LN_EPS = 1e-05
        key = jax.random.key(seed)
        ks = jax.random.split(key, 8)
        B, S, H, A, L = (32, 512, 256, 64, 10)
        return {'hidden_states': jax.random.normal(ks[0], (B, S, H), dtype=jnp.float32), 'language_ids': jax.random.randint(ks[1], (B,), 0, L, dtype=jnp.int64), 'W1': jax.random.normal(ks[2], (L, H, A), dtype=jnp.float32) * (1.0 / np.sqrt(H)), 'b1': jnp.zeros((L, A), dtype=jnp.float32), 'W2': jax.random.normal(ks[3], (L, A, H), dtype=jnp.float32) * (1.0 / np.sqrt(A)), 'b2': jnp.zeros((L, H), dtype=jnp.float32), 'gamma': jnp.ones((L, H), dtype=jnp.float32), 'beta': jnp.zeros((L, H), dtype=jnp.float32)}
    _L1_cond_all = _L1_cond_setup()
    _L1_cond_in = {k: v for k, v in _L1_cond_all.items() if k in ('W1', 'b1', 'W2', 'b2', 'gamma', 'beta')}
    del _L1_cond_all

    def _L1_ffn_setup():
        import jax, jax.numpy as jnp
        import numpy as np
        TOP_K = 2
        EPS = 1e-10
        key = jax.random.key(seed)
        k1, k2, k3, k4 = jax.random.split(key, 4)
        B, S, H, E = (4, 512, 256, 8)
        tokens = jax.random.normal(k1, (B, S, H), dtype=jnp.float32)
        router_w = jax.random.normal(k2, (E, H), dtype=jnp.float32) * (1.0 / np.sqrt(H))
        router_b = jax.random.normal(k3, (E,), dtype=jnp.float32) * 0.01
        expert_weights = jax.random.normal(k4, (E, H, H), dtype=jnp.float32) * (1.0 / np.sqrt(H))
        return {'tokens': tokens, 'router_w': router_w, 'router_b': router_b, 'expert_weights': expert_weights}
    _L1_ffn_all = _L1_ffn_setup()
    _L1_ffn_in = {k: v for k, v in _L1_ffn_all.items() if k in ('router_w', 'router_b', 'expert_weights')}
    del _L1_ffn_all
    return {'x': x, 'itok_B_0_63': itok_B_0_63, 'itok_B_0_8': itok_B_0_8, 'L0_cond_W': _L0_cond_in['W'], 'L0_cond_b': _L0_cond_in['b'], 'L0_ffn_weight': _L0_ffn_in['weight'], 'L0_ffn_aux_weight1': _L0_ffn_in['aux_weight1'], 'L0_ffn_aux_weight2': _L0_ffn_in['aux_weight2'], 'L0_ffn_bias': _L0_ffn_in['bias'], 'L1_cond_W1': _L1_cond_in['W1'], 'L1_cond_b1': _L1_cond_in['b1'], 'L1_cond_W2': _L1_cond_in['W2'], 'L1_cond_b2': _L1_cond_in['b2'], 'L1_cond_gamma': _L1_cond_in['gamma'], 'L1_cond_beta': _L1_cond_in['beta'], 'L1_ffn_router_w': _L1_ffn_in['router_w'], 'L1_ffn_router_b': _L1_ffn_in['router_b'], 'L1_ffn_expert_weights': _L1_ffn_in['expert_weights']}

def reference(x, itok_B_0_63, itok_B_0_8, L0_cond_W, L0_cond_b, L0_ffn_weight, L0_ffn_aux_weight1, L0_ffn_aux_weight2, L0_ffn_bias, L1_cond_W1, L1_cond_b1, L1_cond_W2, L1_cond_b2, L1_cond_gamma, L1_cond_beta, L1_ffn_router_w, L1_ffn_router_b, L1_ffn_expert_weights):
    import jax
    import jax.numpy as jnp

    def _L0_cond_ref(x, cat_ids, W, b):
        import jax, jax.numpy as jnp
        import numpy as np
        NUM_CATEGORIES = 64
        INPUT_DIM = 256
        HIDDEN_DIM = 256
        B = 64
        S = 64
        selected_W = W[cat_ids]
        selected_b = b[cat_ids]
        out = jnp.einsum('bsd,bdh->bsh', x, selected_W) + selected_b[:, None, :]
        return out

    def _L0_ffn_ref(x, weight, aux_weight1, aux_weight2, bias):
        import jax, jax.numpy as jnp
        import numpy as np
        D_MODEL = 256
        h = jnp.einsum('btc,cd->btd', x, weight)
        h = jnp.einsum('btc,cd->btd', h, aux_weight1)
        h = jnp.einsum('btc,cd->btd', h, aux_weight2)
        return jnp.tanh(h + bias)

    def _L1_cond_ref(hidden_states, language_ids, W1, b1, W2, b2, gamma, beta):
        import jax, jax.numpy as jnp
        import numpy as np
        LN_EPS = 1e-05
        w1 = W1[language_ids]
        w2 = W2[language_ids]
        h = jnp.einsum('bsh,bha->bsa', hidden_states, w1) + b1[language_ids][:, None, :]
        h = jax.nn.relu(h)
        adapted = jnp.einsum('bsa,bah->bsh', h, w2) + b2[language_ids][:, None, :]
        x = hidden_states + adapted
        mean = jnp.mean(x, axis=-1, keepdims=True)
        var = jnp.mean(jnp.square(x - mean), axis=-1, keepdims=True)
        normed = (x - mean) * jax.lax.rsqrt(var + LN_EPS)
        return normed * gamma[language_ids][:, None, :] + beta[language_ids][:, None, :]

    def _L1_ffn_ref(tokens, router_w, router_b, expert_weights):
        import jax, jax.numpy as jnp
        import numpy as np
        TOP_K = 2
        EPS = 1e-10
        B, S, H = tokens.shape
        E = expert_weights.shape[0]
        logits = jnp.einsum('bsh,eh->bse', tokens, router_w) + router_b
        probs = jax.nn.softmax(logits, axis=-1)
        top_p, top_i = jax.lax.top_k(probs, TOP_K)
        w = top_p / (jnp.sum(top_p, axis=-1, keepdims=True) + EPS)
        x = tokens.reshape(-1, H)
        idx = top_i.reshape(-1, TOP_K)
        wf = w.reshape(-1, TOP_K)
        y_all = jnp.einsum('nh,ehd->ned', x, expert_weights)
        y_k = jnp.take_along_axis(y_all, idx[:, :, None], axis=1)
        out = jnp.einsum('nk,nkh->nh', wf, y_k)
        acc = jnp.clip(jnp.sum(wf, axis=-1), EPS, None)
        out = (out / acc[:, None]).reshape(B, S, H)
        scale = 1.0 + jnp.sum(w, axis=-1, keepdims=True) * EPS
        return out * scale
    x = x + _L0_ffn_ref(_L0_cond_ref(x, itok_B_0_63, L0_cond_W, L0_cond_b), L0_ffn_weight, L0_ffn_aux_weight1, L0_ffn_aux_weight2, L0_ffn_bias)
    x = x + _L1_ffn_ref(_L1_cond_ref(x, itok_B_0_8, L1_cond_W1, L1_cond_b1, L1_cond_W2, L1_cond_b2, L1_cond_gamma, L1_cond_beta), L1_ffn_router_w, L1_ffn_router_b, L1_ffn_expert_weights)
    return x

_drawn_inputs = setup_inputs


def setup_inputs(seed=0):
    import zlib

    import numpy as np

    out = dict(_drawn_inputs(seed))
    spreads = {'L0_cond_b': (0.0, 0.313),
     'L0_ffn_bias': (0.0, 0.1),
     'L1_cond_b1': (0.0, 0.1),
     'L1_cond_b2': (0.0, 0.1),
     'L1_cond_gamma': (1.0, 0.2),
     'L1_cond_beta': (0.0, 0.1)}
    factors = {}
    for name, (base, spread) in spreads.items():
        noise = np.random.default_rng([zlib.crc32(name.encode()), seed]).standard_normal(out[name].shape)
        drawn = base * np.exp(spread * noise) if base else spread * noise
        out[name] = jnp.asarray(drawn.astype(out[name].dtype))
    for name, factor in factors.items():
        out[name] = (out[name] * factor).astype(out[name].dtype)
    return out
```

```python
from contextlib import ExitStack

import concourse.bass as bass
from concourse import mybir

ALU = mybir.AluOpType
ACT = mybir.ActivationFunctionType
AX = mybir.AxisListType.X
F32 = mybir.dt.float32
F32R = mybir.dt.float32r
I32 = mybir.dt.int32

P = 128
B = 64
S = 64
D = 256
K2 = D // P
HID = 64
NCAT = 64
NLANG = 10
E = 8
TOK = B * S
PAIR = 2
TILES = 4
GB = TILES * PAIR
GT = TILES * P
GROUPS = TOK // GT
CHUNKS = TILES * E // 2
EBANKS = 4
HALVES = 2
LN_EPS = 1e-5
EPS = 1e-10
BIG = 3.0e38

AT = {"h0": (0, 1), "h0T": 3, "x1T": 5, "x1": 8, "aT": 8, "z": 10, "xnT": 12, "logits": 15, "route": 16}


class Group:

    def __init__(self, i, p):
        self.i, self.p, self.g = i, p, 2 * i + p

    def nth(self, per_group, n):
        return self.g * per_group + n

    def before(self, per_group, back=1):
        return (self.g - back + 1) * per_group


def build(nc, xT, cat_ids, lang_ids, L0W, L0b, wT, aux1, aux2, L0bias, W1, b1, W2, b2, gamma, beta,
          routerT, router_b, We, identity, row_mod, rank, out):
    with ExitStack() as ctx:
        def sb(name, shape, dt=F32):
            return ctx.enter_context(nc.sbuf_tensor(name, shape, dt))

        def sem(name):
            return ctx.enter_context(nc.semaphore(name))

        ident = sb("ident", [P, P])
        rowmod = sb("rowmod", [P, 1])
        rank_sb = sb("rank_sb", [P, TILES, E])
        ids_cat = sb("ids_cat", [P, B], I32)
        ids_lang = sb("ids_lang", [P, B], I32)
        is_cat = sb("is_cat", [P, B])
        is_lang = sb("is_lang", [P, B])
        bcat_in = sb("bcat_in", [P, D])
        bcat = sb("bcat", [P, D], F32R)
        b2_in = sb("b2_in", [P, D])
        b2_tab = sb("b2_tab", [P, D], F32R)
        lang_in = sb("lang_in", [NLANG, 2 * D + HID])
        gammaT = sb("gammaT", [P, K2, B])
        betaT = sb("betaT", [P, K2, B])
        b1T = sb("b1T", [P, B // PAIR])
        wT_sb = sb("wT_sb", [P, K2, D])
        aux1_sb = sb("aux1_sb", [P, K2, D])
        aux2_sb = sb("aux2_sb", [P, K2, D])
        m1T = sb("m1T", [P, K2, D])
        comb_hi = sb("comb_hi", [P, K2, D], F32R)
        comb_lo = sb("comb_lo", [P, K2, D], F32R)
        bias_col = sb("bias_col", [P, K2])
        rw = sb("rw", [P, K2, 32])
        rb_col = sb("rb_col", [P, 1])
        we_in = sb("we_in", [P, K2, E, D])
        we_hi = sb("we_hi", [P, K2, E, D], F32R)
        we_lo = sb("we_lo", [P, K2, E, D], F32R)
        minus_half = sb("minus_half", [P, TILES])

        w_cat = [sb(f"w_cat{p}", [P, GB, K2, D]) for p in range(2)]
        xT_sb = [sb(f"xT_sb{p}", [P, K2, GT]) for p in range(2)]
        w1_sb = [sb(f"w1_sb{p}", [P, GB, K2, HID]) for p in range(2)]
        w2_sb = [sb(f"w2_sb{p}", [P, TILES, D]) for p in range(2)]
        oh_cat = sb("oh_cat", [P, GB, S], F32R)
        oh_lang = sb("oh_lang", [P, GB, S], F32R)
        h0 = sb("h0", [P, TILES, D])
        hT_hi = sb("hT_hi", [P, K2, GT], F32R)
        hT_lo = sb("hT_lo", [P, K2, GT], F32R)
        th = sb("th", [P, K2, GT])
        x1T = sb("x1T", [P, K2, GT])
        x1 = [sb(f"x1_{p}", [P, TILES, D]) for p in range(2)]
        aT = sb("aT", [P, TILES, P])
        z = sb("z", [P, TILES, D])
        stats = sb("stats", [P, TILES, 6])
        moments = sb("moments", [P, 7, TILES])
        mean, var_eps = moments[:, 5, :], moments[:, 6, :]
        rstd = sb("rstd", [P, TILES])
        zn = sb("zn", [P, TILES, D])
        gx = sb("gx", [P, K2, GT])
        xnT = sb("xnT", [P, K2, GT])
        xn_hi = [sb(f"xn_hi{p}", [P, K2, GT], F32R) for p in range(2)]
        xn_lo = [sb(f"xn_lo{p}", [P, K2, GT], F32R) for p in range(2)]
        lgT = sb("lgT", [P, P])
        sh = sb("sh", [P, TILES, E])
        ex = sb("ex", [P, TILES, E])
        lg = sb("lg", [P, TILES, E])
        key1 = sb("key1", [P, TILES, E])
        oh1 = sb("oh1", [P, TILES, E])
        sh2 = sb("sh2", [P, TILES, E])
        key2 = sb("key2", [P, TILES, E])
        oh2 = sb("oh2", [P, TILES, E])
        pr = sb("pr", [P, TILES, E])
        small = sb("small", [P, 12, TILES])
        gate = [sb(f"gate{p}", [P, TILES, E]) for p in range(2)]

        pf = [ctx.enter_context(nc.psum_tensor(f"pf{i}", [P, 512], F32)) for i in range(4)]
        pe_bank = [ctx.enter_context(nc.psum_tensor(f"pe{i}", [P, 512], F32)) for i in range(EBANKS)]

        ld_ids, ld_cst, ld_cat, ld_comb, ld_bias, ld_lang, ld_b2, ld_rw, ld_we = (
            sem(n) for n in ("ld_ids", "ld_cst", "ld_cat", "ld_comb", "ld_bias", "ld_lang", "ld_b2",
                                "ld_rw", "ld_we"))
        ld_a = [sem(f"ld_a{p}") for p in range(2)]
        ld_l = [sem(f"ld_l{p}") for p in range(2)]
        stored = [sem(f"stored{p}") for p in range(2)]
        zeroed, oh_small, bcat_hi, bcat_done, b2_hi, b2_done = (
            sem(n) for n in ("zeroed", "oh_small", "bcat_hi", "bcat_done", "b2_hi", "b2_done"))
        sel_mm, sel_done, m1_mm, m1_done, comb_mm, comb_hi_done, comb_done = (
            sem(n) for n in ("sel_mm", "sel_done", "m1_mm", "m1_done", "comb_mm", "comb_hi_done", "comb_done"))
        we_hi_done, we_done = sem("we_hi_done"), sem("we_done")
        mm_h0, mm_h0T, mm_x1T, mm_x1, mm_aT, mm_z, mm_xnT, mm_lgT, mm_lg, mm_y = (
            sem(n) for n in ("mm_h0", "mm_h0T", "mm_x1T", "mm_x1", "mm_aT", "mm_z", "mm_xnT", "mm_lgT",
                             "mm_lg", "mm_y"))
        a_h0, a_hhi, a_th, a_x1, a_lgT, a_xhi, a_exp = (
            sem(n) for n in ("a_h0", "a_hhi", "a_th", "a_x1", "a_lgT", "a_xhi", "a_exp"))
        v_stats, v_mom, v_var, v_seq2 = (sem(n) for n in ("v_stats", "v_mom", "v_var", "v_seq2"))
        v_hlo, v_aT, v_z, v_zn, v_gx, v_xlo, v_lg, v_sh, v_gate, v_y, v_seq = (
            sem(n) for n in ("v_hlo", "v_aT", "v_z", "v_zn", "v_gx", "v_xlo", "v_lg", "v_sh",
                             "v_gate", "v_y", "v_seq"))
        g_ohc, g_ohl, g_x1T, g_rstd, g_xnT = (
            sem(n) for n in ("g_ohc", "g_ohl", "g_x1T", "g_rstd", "g_xnT"))

        A_LOADS, L_LOADS = 16 * (1 + GB), 16 * 2 * GB
        block = ctx.enter_context(nc.Block())

        def tile_of(t):
            return slice(t * P, (t + 1) * P)

        def turns(eng, turn):
            turn(None, Group(0, 0))
            turn(Group(0, 0), Group(0, 1))
            with eng.Fori(0, (GROUPS - 2) // 2) as i:
                turn(Group(i, 1), Group(i + 1, 0))
                turn(Group(i + 1, 0), Group(i + 1, 1))
            turn(Group(GROUPS // 2 - 1, 1), None)

        @block.sync
        def _(sp):
            def load_group(n):
                p = n.p
                if n.first is False:
                    sp.wait_ge(mm_h0, n.before(HALVES, 2))
                    sp.wait_ge(g_x1T, n.before(K2, 2))
                sp.dma_start(xT_sb[p][:, :, :],
                             xT[:, bass.ds(n.g * GT, GT)].rearrange("(k p) t -> p k t", p=P)
                             ).then_inc(ld_a[p], 16)
                for b in range(GB):
                    cat = sp.value_load(ids_cat[0:1, bass.ds(n.g * GB + b, 1)], min_val=0, max_val=NCAT - 1)
                    sp.dma_start(w_cat[p][:, b, :, :],
                                 L0W[bass.ds(cat, 1), :, :].rearrange("o (k p) n -> p (o k) n", p=P)
                                 ).then_inc(ld_a[p], 16)
                for b in range(GB):
                    lang = sp.value_load(ids_lang[0:1, bass.ds(n.g * GB + b, 1)], min_val=0, max_val=NLANG - 1)
                    if b == 0 and n.first is False:
                        sp.wait_ge(mm_z, n.before(HALVES, 2))
                    sp.dma_start(w1_sb[p][:, b, :, :],
                                 W1[bass.ds(lang, 1), :, :].rearrange("o p (k n) -> p (o k) n", k=K2)
                                 ).then_inc(ld_l[p], 16)
                    j = b % PAIR
                    sp.dma_start(w2_sb[p][j * HID:(j + 1) * HID, b // PAIR, :],
                                 W2[bass.ds(lang, 1), :, :].rearrange("o a n -> (o a) n")
                                 ).then_inc(ld_l[p], 16)

            sp.dma_start(ids_cat[:, :], cat_ids).then_inc(ld_ids, 16)
            sp.dma_start(ids_lang[:, :], lang_ids).then_inc(ld_ids, 16)
            sp.wait_ge(ld_ids, 32)
            for p in range(2):
                n = Group(0, p)
                n.first = True
                load_group(n)
            with sp.Fori(1, GROUPS // 2) as i:
                for p in range(2):
                    n = Group(i, p)
                    n.first = False
                    load_group(n)

        @block.tensor
        def _(pe):
            mm, tr = nc.tensor.matmul, nc.tensor.transpose

            pe.wait_ge(ld_lang, 16 * 3)
            pe.wait_ge(oh_small, 2)
            for n in range(2 * K2):
                mm(pe_bank[0][:, n * B:(n + 1) * B], lang_in[:, n * P:(n + 1) * P], is_lang[0:NLANG, :],
                   start=True, stop=True)
            for j in range(PAIR):
                last = mm(pe_bank[0][j * HID:(j + 1) * HID, 4 * B:4 * B + B // PAIR],
                          lang_in[:, 2 * D:2 * D + HID], is_lang[0:NLANG, j:B:PAIR], start=True, stop=True)
            last.then_inc(sel_mm, 1)
            pe.wait_ge(ld_comb, 16 * 3)
            for m in range(K2):
                for k in range(K2):
                    last = mm(pe_bank[1][:, m * D:(m + 1) * D], aux1_sb[:, k, tile_of(m)], wT_sb[:, k, :],
                              start=(k == 0), stop=(k == K2 - 1))
            last.then_inc(m1_mm, 1)

            def combine_weights():
                pe.wait_ge(m1_done, 1)
                for m in range(K2):
                    for k in range(K2):
                        last = mm(pe_bank[2][:, m * D:(m + 1) * D], m1T[:, k, tile_of(m)], aux2_sb[:, k, :],
                                  start=(k == 0), stop=(k == K2 - 1))
                last.then_inc(comb_mm, 1)

            def front(n, s, first):
                p = n.p
                for half in range(HALVES):
                    if s == AT["h0"][half]:
                        if half == 0:
                            pe.wait_ge(g_ohc, n.nth(1, 1))
                            if first:
                                pe.wait_ge(bcat_done, 1)
                            else:
                                pe.wait_ge(v_lg, n.before(1))
                            pe.wait_ge(ld_a[p], (n.i + 1) * A_LOADS)
                        for t in (2 * half, 2 * half + 1):
                            bank = pf[half][:, (t % 2) * D:(t % 2 + 1) * D]
                            mm(bank, oh_cat[:, PAIR * t:PAIR * (t + 1), :].rearrange("p b s -> p (b s)"),
                               bcat[:, :], start=True, stop=False, skip_group_check=True)
                            for k in range(K2):
                                for j in range(PAIR):
                                    b = PAIR * t + j
                                    last = mm(bank[j * S:(j + 1) * S, :], xT_sb[p][:, k, b * S:(b + 1) * S],
                                              w_cat[p][:, b, k, :], start=False, stop=(k == K2 - 1),
                                              skip_group_check=True)
                        last.then_inc(mm_h0, 1)
                if s == AT["h0T"]:
                    pe.wait_ge(a_h0, n.nth(HALVES, HALVES))
                    if first:
                        pe.wait_ge(ld_cst, 16 * 3)
                    for k in range(K2):
                        for t in range(TILES):
                            last = tr(pf[2 + k][:, tile_of(t)], h0[:, t, tile_of(k)], ident[:, :])
                        last.then_inc(mm_h0T, 1)
                    if first:
                        combine_weights()
                if s == AT["x1T"]:
                    if first:
                        pe.wait_ge(comb_done, 1)
                    for m in range(K2):
                        for k in range(K2):
                            if m == 0:
                                pe.wait_ge(a_hhi, n.nth(K2, k + 1))
                            mm(pf[m][:, :], comb_hi[:, k, tile_of(m)], hT_hi[:, k, :], start=(k == 0), stop=False)
                            mm(pf[m][:, :], comb_lo[:, k, tile_of(m)], hT_hi[:, k, :], start=False, stop=False)
                            if m == 0:
                                pe.wait_ge(v_hlo, n.nth(K2, k + 1))
                            last = mm(pf[m][:, :], comb_hi[:, k, tile_of(m)], hT_lo[:, k, :], start=False,
                                      stop=(k == K2 - 1))
                        last.then_inc(mm_x1T, 1)
                if s == AT["x1"]:
                    pe.wait_ge(g_x1T, n.nth(K2, K2))
                    for half in range(HALVES):
                        for t in (2 * half, 2 * half + 1):
                            for k in range(K2):
                                last = tr(pf[2 + half][:, (t % 2) * D + k * P:(t % 2) * D + (k + 1) * P],
                                          x1T[:, k, tile_of(t)], ident[:, :])
                        last.then_inc(mm_x1, 1)
                if s == AT["aT"]:
                    pe.wait_ge(ld_l[p], (n.i + 1) * L_LOADS)
                    for t in range(TILES):
                        for k in range(K2):
                            for j in range(PAIR):
                                b = PAIR * t + j
                                last = mm(pf[0][j * HID:(j + 1) * HID, t * S:(t + 1) * S], w1_sb[p][:, b, k, :],
                                          x1T[:, k, b * S:(b + 1) * S], start=(k == 0), stop=(k == K2 - 1))
                    last.then_inc(mm_aT, 1)
                if s == AT["z"]:
                    pe.wait_ge(g_ohl, n.nth(1, 1))
                    if first:
                        pe.wait_ge(b2_done, 1)
                    pe.wait_ge(v_aT, n.nth(1, 1))
                    for half in range(HALVES):
                        for t in (2 * half, 2 * half + 1):
                            bank = pf[1 - half][:, (t % 2) * D:(t % 2 + 1) * D]
                            mm(bank, oh_lang[:, PAIR * t:PAIR * (t + 1), :].rearrange("p b s -> p (b s)"),
                               b2_tab[:, :], start=True, stop=False)
                            last = mm(bank, aT[:, t, :], w2_sb[p][:, t, :], start=False, stop=True)
                        last.then_inc(mm_z, 1)
                if s == AT["xnT"]:
                    for k in range(K2):
                        if k == 0:
                            pe.wait_ge(v_zn, n.nth(TILES, TILES))
                        for t in range(TILES):
                            last = tr(pf[2 + k][:, tile_of(t)], zn[:, t, tile_of(k)], ident[:, :])
                        last.then_inc(mm_xnT, 1)
                if s == AT["logits"]:
                    pe.wait_ge(g_xnT, n.nth(K2, K2))
                    if first:
                        pe.wait_ge(ld_rw, 16 * (K2 + TILES))
                    for k in range(K2):
                        for t in range(TILES):
                            last = mm(pf[1][32 * t:32 * (t + 1), 0:P], rw[:, k, :], xnT[:, k, tile_of(t)],
                                      start=(k == 0), stop=(k == K2 - 1), tile_position=(0, 32 * t))
                    last.then_inc(mm_lgT, 1)
                if s == AT["route"]:
                    pe.wait_ge(a_lgT, n.nth(1, 1))
                    tr(pf[0][:, 0:P], lgT[:, :], ident[:, :]).then_inc(mm_lg, 1)

            def experts(n, c, first):
                p, t, q = n.p, c // 4, c % 4
                if c == 0:
                    pe.wait_ge(a_xhi, n.nth(K2, K2))
                    pe.wait_ge(v_xlo, n.nth(K2, K2))
                if first:
                    if c == 0:
                        pe.wait_ge(we_done, K2)
                    if c >= EBANKS:
                        pe.wait_ge(v_y, 2 * (c - EBANKS + 1))
                else:
                    pe.wait_ge(v_y, n.nth(E * TILES, 2 * (c - EBANKS + 1)))
                bank = pe_bank[c % EBANKS]
                for k in range(K2):
                    hi, lo = xn_hi[p][:, k, tile_of(t)], xn_lo[p][:, k, tile_of(t)]
                    w_hi = we_hi[:, k, 2 * q:2 * q + 2, :].rearrange("p e n -> p (e n)")
                    w_lo = we_lo[:, k, 2 * q:2 * q + 2, :].rearrange("p e n -> p (e n)")
                    mm(bank[:, :], hi, w_hi, start=(k == 0), stop=False)
                    mm(bank[:, :], hi, w_lo, start=False, stop=False)
                    last = mm(bank[:, :], lo, w_hi, start=False, stop=(k == K2 - 1))
                last.then_inc(mm_y, 1)

            def turn(e, f):
                for s in range(CHUNKS + 1):
                    if f is not None:
                        front(f, s, first=(e is None))
                    if e is not None and s < CHUNKS:
                        experts(e, s, first=(f is not None and e.g is 0))

            turns(pe, turn)

        @block.scalar
        def _(act):
            fn = nc.scalar.activation
            act.dma_start(rowmod[:, :], row_mod).then_inc(ld_cst, 16)
            act.dma_start(bcat_in[0:NCAT, :], L0b).then_inc(ld_cat, 16)
            act.dma_start(bcat_in[NCAT:P, :], L0b).then_inc(ld_cat, 16)
            act.dma_start(ident[:, :], identity).then_inc(ld_cst, 16)
            act.dma_start(rank_sb[:, :, :], rank.rearrange("p (t e) -> p t e", t=TILES)).then_inc(ld_cst, 16)
            for tile, src in ((wT_sb, wT), (aux1_sb, aux1), (aux2_sb, aux2)):
                act.dma_start(tile[:, :, :], src.rearrange("(k p) n -> p k n", p=P)).then_inc(ld_comb, 16)
            for at, src in ((0, gamma), (D, beta), (2 * D, b1)):
                act.dma_start(lang_in[:, at:at + src.shape[1]], src).then_inc(ld_lang, 16)
            act.wait_ge(zeroed, 2)
            for j in range(PAIR):
                act.dma_start(b2_in[j * NCAT:j * NCAT + NLANG, :], b2).then_inc(ld_b2, 16)
            act.dma_start(bias_col[:, :], L0bias).then_inc(ld_bias, 16)
            act.wait_ge(zeroed, 4)
            for k in range(K2):
                act.dma_start(rw[:, k, 0:E], routerT[k * P:(k + 1) * P, :]).then_inc(ld_rw, 16)
            for t in range(TILES):
                act.dma_start(rb_col[32 * t:32 * t + E, :], router_b[:, :]).then_inc(ld_rw, 16)
            for k in range(K2):
                act.dma_start(we_in[:, k, :, :], We[:, k * P:(k + 1) * P, :].rearrange("e p n -> p e n")
                              ).then_inc(ld_we, 16)

            def split_experts(k):
                act.wait_ge(ld_we, 16 * K2)
                fn(we_hi[:, k, :, :], we_in[:, k, :, :], ACT.Copy).then_inc(we_hi_done, 1)

            def front(n, s, first):
                p = n.p
                for half in range(HALVES):
                    if s == AT["h0"][half]:
                        act.wait_ge(mm_h0, n.nth(HALVES, half + 1))
                        if half == 0 and not first:
                            act.wait_ge(mm_h0T, n.before(K2))
                        fn(h0[:, 2 * half:2 * half + 2, :].rearrange("p t n -> p (t n)"), pf[half][:, :], ACT.Copy
                           ).then_inc(a_h0, 1)
                if s == AT["h0T"]:
                    for k in range(K2):
                        act.wait_ge(mm_h0T, n.nth(K2, k + 1))
                        fn(hT_hi[:, k, :], pf[2 + k][:, :], ACT.Copy).then_inc(a_hhi, 1)
                    if first:
                        split_experts(0)
                if s == AT["x1T"]:
                    if first:
                        act.wait_ge(ld_bias, 16)
                    for m in range(K2):
                        act.wait_ge(mm_x1T, n.nth(K2, m + 1))
                        fn(th[:, m, :], pf[m][:, :], ACT.Tanh, bias=bias_col[:, m:m + 1]).then_inc(a_th, 1)
                    if first:
                        split_experts(1)
                if s == AT["x1"]:
                    for half in range(HALVES):
                        act.wait_ge(mm_x1, n.nth(HALVES, half + 1))
                        if half == 0 and waits_store(n):
                            act.wait_ge(stored[p], n.i * 16 * TILES)
                        fn(x1[p][:, 2 * half:2 * half + 2, :].rearrange("p t n -> p (t n)"), pf[2 + half][:, :],
                           ACT.Copy).then_inc(a_x1, 1)
                if s == AT["logits"]:
                    for k in range(K2):
                        act.wait_ge(g_xnT, n.nth(K2, k + 1))
                        if k == 0 and waits_store(n):
                            act.wait_ge(mm_y, n.before(CHUNKS, 2))
                        fn(xn_hi[p][:, k, :], xnT[:, k, :], ACT.Copy).then_inc(a_xhi, 1)
                    act.wait_ge(mm_lgT, n.nth(1, 1))
                    if first:
                        act.wait_ge(ld_rw, 16 * (K2 + TILES))
                    fn(lgT[:, :], pf[1][:, 0:P], ACT.Identity, bias=rb_col[:, 0:1]).then_inc(a_lgT, 1)
                if s == AT["route"]:
                    act.wait_ge(v_sh, n.nth(1, 1))
                    fn(ex[:, :, :], sh[:, :, :], ACT.Exp).then_inc(a_exp, 1)

            def waits_store(n):
                return not (n.i is 0)

            def store(n, t):
                act.wait_ge(v_y, n.nth(E * TILES, E * (t + 1)))
                act.dma_start(out[bass.ds(n.g * GT + t * P, P), :], x1[n.p][:, t, :]).then_inc(stored[n.p], 16)

            def turn(e, f):
                for s in range(CHUNKS + 1):
                    if f is not None:
                        front(f, s, first=(e is None))
                    if e is not None and s in (5, 9, 13):
                        store(e, s // 4 - 1)
                if e is not None:
                    store(e, TILES - 1)

            turns(act, turn)
            for p in range(2):
                act.wait_ge(stored[p], GROUPS // 2 * TILES * 16)

        @block.gpsimd
        def _(pool):
            tt = nc.gpsimd.tensor_tensor
            nc.gpsimd.memset(minus_half[:, :], -0.5).then_inc(zeroed, 1)
            nc.gpsimd.memset(b2_in[:, :], 0.0).then_inc(zeroed, 1)
            nc.gpsimd.memset(rw[:, :, :], 0.0).then_inc(zeroed, 1)
            nc.gpsimd.memset(rb_col[:, :], 0.0).then_inc(zeroed, 1)
            nc.gpsimd.memset(aT[:, :, :], 0.0).then_inc(zeroed, 1)

            def onehots(n, first):
                if first:
                    pool.wait_ge(oh_small, 2)
                else:
                    pool.wait_ge(mm_h0, n.before(HALVES))
                nc.gpsimd.tensor_copy(oh_cat[:, :, :], is_cat[:, bass.ds(n.g * GB, GB)].unsqueeze(2)
                                      .broadcast_to([P, GB, S])).then_inc(g_ohc, 1)
                if not first:
                    pool.wait_ge(mm_z, n.before(HALVES))
                nc.gpsimd.tensor_copy(oh_lang[:, :, :], is_lang[:, bass.ds(n.g * GB, GB)].unsqueeze(2)
                                      .broadcast_to([P, GB, S])).then_inc(g_ohl, 1)

            def turn(e, f):
                n, first = f, e is None
                if n is None:
                    return
                onehots(n, first)
                pool.wait_ge(ld_a[n.p], (n.i + 1) * A_LOADS)
                for m in range(K2):
                    pool.wait_ge(a_th, n.nth(K2, m + 1))
                    if m == 0 and not first:
                        pool.wait_ge(mm_aT, n.before(1))
                    tt(x1T[:, m, :], th[:, m, :], xT_sb[n.p][:, m, :], ALU.add).then_inc(g_x1T, 1)
                if not first:
                    pool.wait_ge(v_zn, n.before(TILES))
                pool.wait_ge(v_var, n.nth(1, 1))
                tt(rstd[:, :], var_eps, minus_half[:, :], ALU.pow).then_inc(g_rstd, 1)
                for k in range(K2):
                    pool.wait_ge(v_gx, n.nth(K2, k + 1))
                    if first:
                        pool.wait_ge(sel_done, 3)
                    elif k == 0:
                        pool.wait_ge(mm_lgT, n.before(1))
                        pool.wait_ge(a_xhi, n.before(K2))
                        pool.wait_ge(v_xlo, n.before(K2))
                    tt(xnT[:, k, :].rearrange("p (b s) -> p b s", s=S),
                       gx[:, k, :].rearrange("p (b s) -> p b s", s=S),
                       betaT[:, k, bass.ds(n.g * GB, GB)].unsqueeze(2).broadcast_to([P, GB, S]), ALU.add
                       ).then_inc(g_xnT, 1)

            turns(pool, turn)

        @block.vector
        def _(dve):
            tt, ts, stt, red = (nc.vector.tensor_tensor, nc.vector.tensor_scalar,
                                nc.vector.scalar_tensor_tensor, nc.vector.tensor_reduce)
            SEQ = 17

            dve.wait_ge(ld_ids, 32)
            dve.wait_ge(ld_cst, 16 * 3)
            ts(is_cat[:, :], ids_cat[:, :], rowmod[:, 0:1], None, ALU.is_equal).then_inc(oh_small, 1)
            ts(is_lang[:, :], ids_lang[:, :], rowmod[:, 0:1], None, ALU.is_equal).then_inc(oh_small, 1)

            def split_table(dst, src, hi, done):
                nc.vector.tensor_copy(dst[:, :], src[:, :]).then_inc(hi, 1)
                dve.wait_ge(hi, 1)
                tt(dst[NCAT:P, :], src[NCAT:P, :], dst[NCAT:P, :].bitcast(F32), ALU.subtract).then_inc(done, 1)

            dve.wait_ge(ld_cat, 32)
            split_table(bcat, bcat_in, bcat_hi, bcat_done)
            dve.wait_ge(ld_b2, 16 * 2)
            split_table(b2_tab, b2_in, b2_hi, b2_done)
            dve.wait_ge(sel_mm, 1)
            nc.vector.tensor_copy(gammaT[:, :, :].rearrange("p k b -> p (k b)"), pe_bank[0][:, 0:2 * B]
                                  ).then_inc(sel_done, 1)
            nc.vector.tensor_copy(betaT[:, :, :].rearrange("p k b -> p (k b)"), pe_bank[0][:, 2 * B:4 * B]
                                  ).then_inc(sel_done, 1)
            nc.vector.tensor_copy(b1T[:, :], pe_bank[0][:, 4 * B:4 * B + B // PAIR]).then_inc(sel_done, 1)
            dve.wait_ge(m1_mm, 1)
            nc.vector.tensor_copy(m1T[:, :, :].rearrange("p k n -> p (k n)"), pe_bank[1][:, :]).then_inc(m1_done, 1)

            def split_experts(k):
                dve.wait_ge(we_hi_done, k + 1)
                tt(we_lo[:, k, :, :], we_in[:, k, :, :], we_hi[:, k, :, :].bitcast(F32), ALU.subtract
                   ).then_inc(we_done, 1)

            def route(n, first):
                p = n.p
                step = [0]

                def seq(ins):
                    step[0] += 1
                    ins.then_inc(v_seq, 1)
                    dve.wait_ge(v_seq, n.nth(SEQ, step[0]))

                def wide(i):
                    return small[:, i, :].unsqueeze(2).broadcast_to([P, TILES, E])

                dve.wait_ge(mm_lg, n.nth(1, 1))
                nc.vector.tensor_copy(lg[:, :, :], pf[0][:, 0:P].rearrange("p (t c) -> p t c", t=TILES)[:, :, 0:E]
                                      ).then_inc(v_lg, 1)
                dve.wait_ge(v_lg, n.nth(1, 1))
                seq(red(small[:, 0, :], lg[:, :, :], AX, ALU.max))
                tt(sh[:, :, :], lg[:, :, :], wide(0), ALU.subtract).then_inc(v_sh, 1)
                dve.wait_ge(v_sh, n.nth(1, 1))
                seq(stt(key1[:, :, :], sh[:, :, :], 0.0, rank_sb[:, :, :], ALU.is_equal, ALU.mult))
                seq(red(small[:, 1, :], key1[:, :, :], AX, ALU.max))
                seq(tt(oh1[:, :, :], key1[:, :, :], wide(1), ALU.is_equal))
                seq(stt(sh2[:, :, :], oh1[:, :, :], -BIG, sh[:, :, :], ALU.mult, ALU.add))
                seq(red(small[:, 2, :], sh2[:, :, :], AX, ALU.max))
                seq(tt(key2[:, :, :], sh2[:, :, :], wide(2), ALU.is_equal))
                seq(tt(key2[:, :, :], key2[:, :, :], rank_sb[:, :, :], ALU.mult))
                seq(red(small[:, 3, :], key2[:, :, :], AX, ALU.max))
                seq(tt(oh2[:, :, :], key2[:, :, :], wide(3), ALU.is_equal))
                seq(tt(oh2[:, :, :], oh2[:, :, :], oh1[:, :, :], ALU.add))
                dve.wait_ge(a_exp, n.nth(1, 1))
                seq(red(small[:, 4, :], ex[:, :, :], AX, ALU.add))
                seq(nc.vector.reciprocal(small[:, 5, :], small[:, 4, :]))
                seq(tt(pr[:, :, :], ex[:, :, :], wide(5), ALU.mult))
                seq(tt(pr[:, :, :], pr[:, :, :], oh2[:, :, :], ALU.mult))
                seq(red(small[:, 6, :], pr[:, :, :], AX, ALU.add))
                seq(ts(small[:, 7, :], small[:, 6, :], EPS, None, ALU.add))
                assert step[0] == SEQ
                route2(n)

            SEQ2 = 7

            def route2(n):
                p = n.p
                step = [0]

                def seq(ins):
                    step[0] += 1
                    ins.then_inc(v_seq2, 1)
                    dve.wait_ge(v_seq2, n.nth(SEQ2, step[0]))

                def wide(i):
                    return small[:, i, :].unsqueeze(2).broadcast_to([P, TILES, E])

                seq(nc.vector.reciprocal(small[:, 8, :], small[:, 7, :]))
                seq(tt(pr[:, :, :], pr[:, :, :], wide(8), ALU.mult))
                seq(red(small[:, 9, :], pr[:, :, :], AX, ALU.add))
                seq(ts(small[:, 10, :], small[:, 9, :], EPS, None, ALU.max))
                seq(nc.vector.reciprocal(small[:, 11, :], small[:, 10, :]))
                seq(ts(small[:, 10, :], small[:, 9, :], EPS, 1.0, ALU.mult, ALU.add))
                seq(tt(small[:, 11, :], small[:, 11, :], small[:, 10, :], ALU.mult))
                tt(gate[p][:, :, :], pr[:, :, :], wide(11), ALU.mult).then_inc(v_gate, 1)


            def front(n, s, first):
                p = n.p
                if s == AT["h0T"]:
                    for k in range(K2):
                        dve.wait_ge(a_hhi, n.nth(K2, k + 1))
                        tt(hT_lo[:, k, :], pf[2 + k][:, :], hT_hi[:, k, :].bitcast(F32), ALU.subtract
                           ).then_inc(v_hlo, 1)
                    if first:
                        dve.wait_ge(comb_mm, 1)
                        nc.vector.tensor_copy(comb_hi[:, :, :].rearrange("p k n -> p (k n)"), pe_bank[2][:, :]
                                              ).then_inc(comb_hi_done, 1)
                        dve.wait_ge(comb_hi_done, 1)
                        tt(comb_lo[:, :, :].rearrange("p k n -> p (k n)"), pe_bank[2][:, :],
                           comb_hi[:, :, :].rearrange("p k n -> p (k n)").bitcast(F32), ALU.subtract
                           ).then_inc(comb_done, 1)
                if s == AT["aT"]:
                    if first:
                        dve.wait_ge(zeroed, 5)
                        dve.wait_ge(sel_done, 3)
                    dve.wait_ge(mm_aT, n.nth(1, 1))
                    for t in range(TILES):
                        for j in range(PAIR):
                            rows = slice(j * HID, (j + 1) * HID)
                            last = ts(aT[rows, t, j * S:(j + 1) * S], pf[0][rows, t * S:(t + 1) * S],
                                      b1T[rows, bass.ds(n.g * TILES + t, 1)], 0.0, ALU.add, ALU.max)
                    last.then_inc(v_aT, 1)
                if s == AT["z"]:
                    if first:
                        split_experts(0)
                    for half in range(HALVES):
                        dve.wait_ge(mm_z, n.nth(HALVES, half + 1))
                        dve.wait_ge(a_x1, n.nth(HALVES, half + 1))
                        tiles = slice(2 * half, 2 * half + 2)
                        tt(z[:, tiles, :].rearrange("p t n -> p (t n)"), pf[1 - half][:, :],
                           x1[p][:, tiles, :].rearrange("p t n -> p (t n)"), ALU.add).then_inc(v_z, 1)
                    for t in range(TILES):
                        dve.wait_ge(v_z, n.nth(HALVES, t // 2 + 1))
                        nc.vector.bn_stats(stats[:, t, :], z[:, t, :]).then_inc(v_stats, 1)
                    mean_e, mean_o, m2_e, m2_o = (stats[:, :, c] for c in (1, 4, 2, 5))
                    dve.wait_ge(v_stats, n.nth(TILES, TILES))
                    tt(moments[:, 0, :], mean_e, mean_o, ALU.add).then_inc(v_mom, 1)
                    tt(moments[:, 1, :], mean_e, mean_o, ALU.subtract).then_inc(v_mom, 1)
                    tt(moments[:, 2, :], m2_e, m2_o, ALU.add).then_inc(v_mom, 1)
                    dve.wait_ge(v_mom, n.nth(6, 3))
                    stt(moments[:, 3, :], moments[:, 1, :], 0.25, moments[:, 1, :], ALU.mult, ALU.mult
                        ).then_inc(v_mom, 1)
                    ts(moments[:, 4, :], moments[:, 2, :], 1.0 / D, LN_EPS, ALU.mult, ALU.add).then_inc(v_mom, 1)
                    ts(mean, moments[:, 0, :], 0.5, None, ALU.mult).then_inc(v_mom, 1)
                    dve.wait_ge(v_mom, n.nth(6, 6))
                    tt(var_eps, moments[:, 3, :], moments[:, 4, :], ALU.add).then_inc(v_var, 1)
                if s == AT["xnT"] - 1:
                    dve.wait_ge(g_rstd, n.nth(1, 1))
                    if not first:
                        dve.wait_ge(mm_xnT, n.before(K2))
                    for t in range(TILES):
                        ts(zn[:, t, :], z[:, t, :], moments[:, 5, t:t + 1], rstd[:, t:t + 1], ALU.subtract, ALU.mult
                           ).then_inc(v_zn, 1)
                if s == AT["xnT"]:
                    if not first:
                        dve.wait_ge(g_xnT, n.before(K2))
                    for k in range(K2):
                        dve.wait_ge(mm_xnT, n.nth(K2, k + 1))
                        tt(gx[:, k, :].rearrange("p (b s) -> p b s", s=S),
                           pf[2 + k][:, :].rearrange("p (b s) -> p b s", s=S),
                           gammaT[:, k, bass.ds(n.g * GB, GB)].unsqueeze(2).broadcast_to([P, GB, S]), ALU.mult
                           ).then_inc(v_gx, 1)
                    if first:
                        split_experts(1)
                if s == AT["logits"]:
                    for k in range(K2):
                        dve.wait_ge(a_xhi, n.nth(K2, k + 1))
                        tt(xn_lo[p][:, k, :], xnT[:, k, :], xn_hi[p][:, k, :].bitcast(F32), ALU.subtract
                           ).then_inc(v_xlo, 1)
                if s == AT["route"]:
                    route(n, first)

            def experts(n, c):
                p, t, q = n.p, c // 4, c % 4
                if c == 0:
                    dve.wait_ge(v_gate, n.nth(1, 1))
                dve.wait_ge(mm_y, n.nth(CHUNKS, c + 1))
                for h in range(2):
                    e = 2 * q + h
                    if e > 0:
                        dve.wait_ge(v_y, n.nth(E * TILES, c * 2 + h))
                    ins = stt(x1[p][:, t, :], pe_bank[c % EBANKS][:, h * D:(h + 1) * D],
                              gate[p][:, t, e:e + 1], x1[p][:, t, :], ALU.mult, ALU.add)
                    ins.then_inc(v_y, 1)


            def turn(e, f):
                for s in range(CHUNKS + 1):
                    if f is not None:
                        front(f, s, first=(e is None))
                    if e is not None and s < CHUNKS:
                        experts(e, s)

            turns(dve, turn)


def kernel(x, itok_B_0_63, itok_B_0_8, L0_cond_W, L0_cond_b, L0_ffn_weight, L0_ffn_aux_weight1,
           L0_ffn_aux_weight2, L0_ffn_bias, L1_cond_W1, L1_cond_b1, L1_cond_W2, L1_cond_b2,
           L1_cond_gamma, L1_cond_beta, L1_ffn_router_w, L1_ffn_router_b, L1_ffn_expert_weights):
    import numpy as np
    import concourse.bacc as bacc
    from concourse.bass_utils import run_bass_kernel_spmd

    def lay(a):
        return np.ascontiguousarray(a)

    arrays = {
        "xT": lay(np.asarray(x).reshape(TOK, D).T),
        "cat_ids": lay(np.broadcast_to(np.asarray(itok_B_0_63).reshape(1, B), (P, B))),
        "lang_ids": lay(np.broadcast_to(np.asarray(itok_B_0_8).reshape(1, B), (P, B))),
        "L0W": lay(L0_cond_W),
        "L0b": lay(L0_cond_b),
        "wT": lay(np.asarray(L0_ffn_weight).T),
        "aux1": lay(L0_ffn_aux_weight1),
        "aux2": lay(L0_ffn_aux_weight2),
        "L0bias": lay(np.asarray(L0_ffn_bias).reshape(K2, P).T),
        "W1": lay(np.asarray(L1_cond_W1).reshape(NLANG, K2, P, HID).transpose(0, 2, 1, 3)
                  .reshape(NLANG, P, K2 * HID)),
        "b1": lay(L1_cond_b1),
        "W2": lay(L1_cond_W2),
        "b2": lay(L1_cond_b2),
        "gamma": lay(L1_cond_gamma),
        "beta": lay(L1_cond_beta),
        "routerT": lay(np.asarray(L1_ffn_router_w).T),
        "router_b": lay(np.asarray(L1_ffn_router_b).reshape(E, 1)),
        "We": lay(L1_ffn_expert_weights),
        "identity": np.eye(P, dtype=np.float32),
        "row_mod": (np.arange(P) % NCAT).astype(np.float32).reshape(P, 1),
        "rank": np.tile(np.arange(E, 0, -1).astype(np.float32), (P, TILES)),
    }
    nc = bacc.Bacc("TRN2", target_bir_lowering=False, num_devices=1)
    args = {name: nc.dram_tensor(name, a.shape, mybir.dt.from_np(a.dtype), kind="ExternalInput").ap()
            for name, a in arrays.items()}
    args["out"] = nc.dram_tensor("out", (TOK, D), F32, kind="ExternalOutput").ap()
    build(nc, **args)
    r = run_bass_kernel_spmd(nc, [arrays], core_ids=[0])
    return r.results[0]["out"].reshape(B, S, D)
```

```python
from contextlib import ExitStack

import concourse.bass as bass
from concourse import mybir

ALU = mybir.AluOpType
ACT = mybir.ActivationFunctionType
AX = mybir.AxisListType.X
F32 = mybir.dt.float32
F32R = mybir.dt.float32r
I32 = mybir.dt.int32

P = 128
B = 64
S = 64
D = 256
K2 = D // P
HID = 64
NCAT = 64
NLANG = 10
E = 8
TOK = B * S
PAIR = 2
TILES = 4
GB = TILES * PAIR
GT = TILES * P
GROUPS = TOK // GT
CHUNKS = TILES * E // 2
EBANKS = 4
HALVES = 2
HEAD = P + 1 + TILES * E + D
TAIL = 3 * D + HID + K2 + 1 + K2 * 32
LN_EPS = 1e-5
EPS = 1e-10
BIG = 3.0e38
LAG = 3



class Group:

    def __init__(self, i, p, early=False):
        self.i, self.p, self.g = i, p, 2 * i + p
        self.early, self.first = early, early and self.g == 0
        self.second = early and self.g == 1

    def nth(self, per_group, n):
        return self.g * per_group + n

    def before(self, per_group, back=1):
        return (self.g - back + 1) * per_group

    def loads(self, per_group):
        return (self.i + 1) * per_group


def start_up():
    a, b, c = Group(0, 0, early=True), Group(0, 1, early=True), Group(1, 0)
    yield from (("prepare", a), ("onehots", a), ("onehots", b), ("combine1", a), ("h0", a, 0), ("combine2", a), ("h0", a, 1), ("select", a), ("h0T", a), ("adapter", a, 0), ("x1T", a), ("adapter", a, 1), ("adapter_v", a, 2), ("h0", b, 0), ("adapter_v", a, 3), ("x1", a), ("split_we", a, 0), ("h0", b, 1), ("aT", a), ("h0T", b), ("split_we", a, 1), ("z", a), ("zn", a), ("x1T", b), ("adapter", b, 0), ("xnT", a), ("split_we", a, 3), ("adapter", b, 1), ("adapter", b, 2), ("split_we", a, 2), ("split_xn", a), ("logits", a), ("x1", b), ("adapter", b, 3), ("route", a))
    yield from experts(a, {2: (("aT", b),), 10: (("z", b),), 14: (("zn", b),), 21: (("onehots", c),), 25: (("xnT", b), ("split_xn", b),)}, 0)
    yield ("logits", b)


def experts(e, front, lag):
    for c in range(CHUNKS + lag):
        yield from front.get(2 * c, ())
        if c < CHUNKS:
            yield ("y", e, c)
        yield from front.get(2 * c + 1, ())
        if c >= lag:
            yield ("add", e, c - lag)
            done = c - lag - 2
            if done % 4 == 3 and 0 < done < CHUNKS - 4:
                yield ("store", e, done // 4)
        if c == 1 and not e.first:
            yield ("store_last", e)


def turn(e, f, after):
    yield from experts(e, {0: (("route", e),)} if f is None else
        {0: (("h0", f, 0), ("route", e),), 2: (("adapter", f, 0),), 4: (("h0", f, 1), ("adapter", f, 1),), 5: (("h0T", f),), 8: (("adapter", f, 3),), 10: (("x1T", f),), 14: (("adapter", f, 2), ("x1", f), ("aT", f),), 16: (("z", f),), 23: (("zn", f),), 25: (("onehots", after),), 27: (("xnT", f),), 29: (("split_xn", f),)}, 0)
    if f is not None:
        yield ("logits", f)


def build(nc, xT, ids, head, L0W, L0_mats, tail, W1, W2, We, out):
    with ExitStack() as ctx:
        def sb(name, shape, dt=F32):
            return ctx.enter_context(nc.sbuf_tensor(name, shape, dt))

        def sem(name):
            return ctx.enter_context(nc.semaphore(name))

        head_in = sb("head_in", [P, HEAD])
        ident, rowmod = head_in[:, 0:P], head_in[:, P:P + 1]
        rank_sb = head_in[:, P + 1:P + 1 + TILES * E].rearrange("p (t e) -> p t e", t=TILES)
        bcat_in = head_in[:, HEAD - D:HEAD]
        tail_in = sb("tail_in", [P, TAIL])
        lang_in, b2_in = tail_in[0:NLANG, 0:2 * D + HID], tail_in[:, 2 * D + HID:3 * D + HID]
        bias_col = tail_in[:, 3 * D + HID:3 * D + HID + K2]
        rb_col = tail_in[:, TAIL - K2 * 32 - 1:TAIL - K2 * 32]
        rw = tail_in[:, TAIL - K2 * 32:TAIL].rearrange("p (k e) -> p k e", k=K2)
        ids_in = sb("ids_in", [P, 2, B], I32)
        is_cat = sb("is_cat", [P, B + GB])
        is_lang = sb("is_lang", [P, B + GB])
        bcat = sb("bcat", [P, D], F32R)
        b2_tab = sb("b2_tab", [P, D], F32R)
        gammaT = sb("gammaT", [P, K2, B])
        betaT = sb("betaT", [P, K2, B])
        b1T = sb("b1T", [P, B // PAIR])
        mats = sb("mats", [P, 3, K2, D])
        m1T = sb("m1T", [P, K2, D])
        comb_hi = sb("comb_hi", [P, K2, D], F32R)
        comb_lo = sb("comb_lo", [P, K2, D], F32R)
        w1_tab = sb("w1_tab", [P, NLANG, K2 * HID])
        w2_tab = sb("w2_tab", [HID, NLANG, D])
        we_in = sb("we_in", [P, E // 2, K2, 2 * D])
        we_hi = sb("we_hi", [P, E // 2, K2, 2 * D], F32R)
        we_lo = sb("we_lo", [P, E // 2, K2, 2 * D], F32R)
        minus_half = sb("minus_half", [P, TILES])
        warm = sb("warm", [P, 1])

        w_cat = [sb(f"w_cat{p}", [P, GB, K2, D]) for p in range(2)]
        xT_sb = [sb(f"xT_sb{p}", [P, K2, GT]) for p in range(2)]
        w1_sb = sb("w1_sb", [P, GB, K2 * HID])
        w2_sb = sb("w2_sb", [P, TILES, D])
        oh_cat = [sb(f"oh_cat{p}", [P, GB, S], F32R) for p in range(2)]
        oh_lang = [sb(f"oh_lang{p}", [P, GB, S], F32R) for p in range(2)]
        h0 = sb("h0", [P, TILES, D])
        hT_hi = sb("hT_hi", [P, K2, GT], F32R)
        hT_lo = sb("hT_lo", [P, K2, GT], F32R)
        th = sb("th", [P, K2, GT])
        x1T = sb("x1T", [P, K2, GT])
        x1 = [sb(f"x1_{p}", [P, TILES, D]) for p in range(2)]
        aT = sb("aT", [P, TILES, P])
        z = sb("z", [P, TILES, D])
        stats = sb("stats", [P, TILES, 6])
        moments = sb("moments", [P, 7, TILES])
        mean, var_eps = moments[:, 5, :], moments[:, 6, :]
        rstd = sb("rstd", [P, TILES])
        zn = sb("zn", [P, TILES, D])
        gx = sb("gx", [P, K2, GT])
        xnT = sb("xnT", [P, K2, GT])
        xn_hi = [sb(f"xn_hi{p}", [P, K2, GT], F32R) for p in range(2)]
        xn_lo = [sb(f"xn_lo{p}", [P, K2, GT], F32R) for p in range(2)]
        lgT = sb("lgT", [P, P])
        sh = sb("sh", [P, TILES, E])
        ex = sb("ex", [P, TILES, E])
        key1 = sb("key1", [P, TILES, E])
        oh1 = sb("oh1", [P, TILES, E])
        sh2 = sb("sh2", [P, TILES, E])
        key2 = sb("key2", [P, TILES, E])
        oh2 = sb("oh2", [P, TILES, E])
        pr = sb("pr", [P, TILES, E])
        small = sb("small", [P, 12, TILES])
        gate = [sb(f"gate{p}", [P, TILES, E]) for p in range(2)]

        pf = [ctx.enter_context(nc.psum_tensor(f"pf{i}", [P, 512], F32)) for i in range(4)]
        pe_bank = [ctx.enter_context(nc.psum_tensor(f"pe{i}", [P, 512], F32)) for i in range(EBANKS)]

        ld_ids, ld_head, ld_mats, ld_tail, ld_tabs = (
            sem(n) for n in ("ld_ids", "ld_head", "ld_mats", "ld_tail", "ld_tabs"))
        ld_a = [sem(f"ld_a{p}") for p in range(2)]
        ld_b = [sem(f"ld_b{p}") for p in range(2)]
        ld_we = [sem(f"ld_we{q}") for q in range(E // 2)]
        stored = [sem(f"stored{p}") for p in range(2)]
        zeroed, oh_small, bcat_hi, bcat_done, b2_hi, b2_done = (
            sem(n) for n in ("zeroed", "oh_small", "bcat_hi", "bcat_done", "b2_hi", "b2_done"))
        sel_mm, sel_done, m1_mm, m1_done, comb_mm, comb_hi_done, comb_done = (
            sem(n) for n in ("sel_mm", "sel_done", "m1_mm", "m1_done", "comb_mm", "comb_hi_done", "comb_done"))
        we_hi_done = [sem(f"we_hi_done{q}") for q in range(E // 2)]
        we_done = [sem(f"we_done{q}") for q in range(E // 2)]
        mm_h0, mm_h0T, mm_x1T, mm_x1, mm_aT, mm_z, mm_xnT, mm_lgT, mm_lg, mm_y = (
            sem(n) for n in ("mm_h0", "mm_h0T", "mm_x1T", "mm_x1", "mm_aT", "mm_z", "mm_xnT", "mm_lgT",
                             "mm_lg", "mm_y"))
        a_h0, a_hhi, w_ready, a_th, a_aT, a_x1, a_lgT, a_xhi, a_exp = (
            sem(n) for n in ("a_h0", "a_hhi", "w_ready", "a_th", "a_aT", "a_x1", "a_lgT", "a_xhi", "a_exp"))
        warm_set, aT_zeroed, v_stats, v_mom, v_var, v_xnT, v_total, v_scale = (
            sem(n) for n in ("warm_set", "aT_zeroed", "v_stats", "v_mom", "v_var", "v_xnT", "v_total", "v_scale"))
        v_hlo, v_aT, v_z, v_zn, v_gx, v_xlo, v_sh, v_gate, v_y, v_seq = (
            sem(n) for n in ("v_hlo", "v_aT", "v_z", "v_zn", "v_gx", "v_xlo", "v_sh",
                             "v_gate", "v_y", "v_seq"))
        g_ohc, g_ohl, g_x1T, g_rstd, g_xnT = (
            sem(n) for n in ("g_ohc", "g_ohl", "g_x1T", "g_rstd", "g_xnT"))

        A_LOADS, B_LOADS = 16 * (1 + GB // 2), 16 * (GB // 2)
        block = ctx.enter_context(nc.Block())

        def row_bank(n, i):
            return pe_bank[i] if n.second else pf[i]

        def col_bank(n, k):
            return pe_bank[2 + k] if n.second else pf[2 + k]

        def adapter(eng, copy, n, t, first):
            for j in range(PAIR):
                b = PAIR * t + j
                lang = eng.value_load(ids_in[0:1, 1, bass.ds(n.g * GB + b, 1)], min_val=0, max_val=NLANG - 1)
                if first and j == 0:
                    if n.first:
                        eng.wait_ge(ld_tabs, 16 * 2)
                    else:
                        eng.wait_ge(mm_z, n.before(HALVES))
                copy(w1_sb[:, b, :], w1_tab[:, bass.ds(lang, 1), :].rearrange("p l n -> p (l n)"))
                last = copy(w2_sb[j * HID:(j + 1) * HID, t, :],
                            w2_tab[:, bass.ds(lang, 1), :].rearrange("p l n -> p (l n)"))
            last.then_inc(w_ready, 1)

        def tile_of(t):
            return slice(t * P, (t + 1) * P)

        def flat(ap):
            return ap.rearrange("p a n -> p (a n)")

        def by_batch(ap):
            return ap.rearrange("p (b s) -> p b s", s=S)

        def run(eng, stages):
            def walk(items):
                for name, n, *more in items:
                    if name in stages:
                        stages[name](n, *more)

            walk(start_up())
            with eng.Fori(0, (GROUPS - 2) // 2) as i:
                walk(turn(Group(i, 1), Group(i + 1, 0), Group(i + 1, 1)))
                walk(turn(Group(i + 1, 0), Group(i + 1, 1), Group(i + 2, 0)))
            walk(turn(Group(GROUPS // 2 - 1, 1), None, None))

        @block.sync
        def _(sp):
            def load_x(n):
                sp.dma_start(xT_sb[n.p][:, :, :],
                             xT[:, bass.ds(n.g * GT, GT)].rearrange("(k p) t -> p k t", p=P)
                             ).then_inc(ld_a[n.p], 16)

            def load_cat(n):
                for b in range(GB):
                    cat = sp.value_load(ids_in[0:1, 0, bass.ds(n.g * GB + b, 1)], min_val=0, max_val=NCAT - 1)
                    sp.dma_start(w_cat[n.p][:, b, :, :],
                                 L0W[bass.ds(cat, 1), :, :].rearrange("o (k p) n -> p (o k) n", p=P)
                                 ).then_inc(ld_a[n.p] if b < GB // 2 else ld_b[n.p], 16)

            a, b = Group(0, 0, early=True), Group(0, 1, early=True)
            sp.dma_start(ids_in[:, :, :], ids.rearrange("p (a b) -> p a b", a=2)).then_inc(ld_ids, 16)
            sp.dma_start(head_in[:, :], head).then_inc(ld_head, 16)
            sp.dma_start(mats[:, :, :, :].rearrange("p m k n -> p (m k n)"), L0_mats).then_inc(ld_mats, 16)
            load_x(a)
            sp.wait_ge(ld_ids, 16)
            load_cat(a)
            sp.dma_start(tail_in[:, :], tail).then_inc(ld_tail, 16)
            sp.dma_start(w1_tab[:, :, :], W1.rearrange("l p n -> p l n")).then_inc(ld_tabs, 16)
            sp.dma_start(w2_tab[:, :, :], W2.rearrange("l a n -> a l n")).then_inc(ld_tabs, 16)
            load_x(b)
            load_cat(b)
            for q in range(E // 2):
                for k in range(K2):
                    sp.dma_start(we_in[:, q, k, :].rearrange("p (e n) -> p e n", n=D),
                                 We[2 * q:2 * q + 2, k * P:(k + 1) * P, :].rearrange("e p n -> p e n")
                                 ).then_inc(ld_we[q], 16)
            with sp.Fori(1, GROUPS // 2) as i:
                for p in range(2):
                    n = Group(i, p)
                    sp.wait_ge(mm_h0, n.before(HALVES, 2))
                    sp.wait_ge(g_x1T, n.before(K2, 2))
                    load_x(n)
                    load_cat(n)

        @block.tensor
        def _(pe):
            mm, tr = nc.tensor.matmul, nc.tensor.transpose

            def select(n):
                pe.wait_ge(ld_tail, 16)
                for m in range(2 * K2):
                    mm(pe_bank[3][:, m * B:(m + 1) * B], lang_in[:, m * P:(m + 1) * P], is_lang[0:NLANG, 0:B],
                       start=True, stop=True)
                for j in range(PAIR):
                    last = mm(pe_bank[3][j * HID:(j + 1) * HID, 4 * B:4 * B + B // PAIR],
                              lang_in[:, 2 * D:2 * D + HID], is_lang[0:NLANG, j:B:PAIR], start=True, stop=True)
                last.then_inc(sel_mm, 1)

            def combine1(n):
                pe.wait_ge(ld_mats, 16)
                for m in range(K2):
                    for k in range(K2):
                        last = mm(pe_bank[1][:, m * D:(m + 1) * D], mats[:, 1, k, tile_of(m)], mats[:, 0, k, :],
                                  start=(k == 0), stop=(k == K2 - 1))
                last.then_inc(m1_mm, 1)

            def combine2(n):
                pe.wait_ge(m1_done, 1)
                for m in range(K2):
                    for k in range(K2):
                        last = mm(pe_bank[2][:, m * D:(m + 1) * D], m1T[:, k, tile_of(m)], mats[:, 2, k, :],
                                  start=(k == 0), stop=(k == K2 - 1))
                last.then_inc(comb_mm, 1)

            def h0_(n, half):
                if half == 0:
                    pe.wait_ge(g_ohc, n.nth(1, 1))
                    if n.first:
                        pe.wait_ge(bcat_done, 1)
                    elif not n.second:
                        pe.wait_ge(v_z, n.before(HALVES))
                    pe.wait_ge(ld_a[n.p], n.loads(A_LOADS))
                else:
                    if not n.early:
                        pe.wait_ge(v_sh, n.before(1))
                    pe.wait_ge(ld_b[n.p], n.loads(B_LOADS))
                for t in (2 * half, 2 * half + 1):
                    bank = row_bank(n, half)[:, (t % 2) * D:(t % 2 + 1) * D]
                    mm(bank, flat(oh_cat[n.p][:, PAIR * t:PAIR * (t + 1), :]), bcat[:, :], start=True, stop=False,
                       skip_group_check=True)
                    for k in range(K2):
                        for j in range(PAIR):
                            b = PAIR * t + j
                            last = mm(bank[j * S:(j + 1) * S, :], xT_sb[n.p][:, k, b * S:(b + 1) * S],
                                      w_cat[n.p][:, b, k, :], start=False, stop=(k == K2 - 1),
                                      skip_group_check=True)
                last.then_inc(mm_h0, 1)

            def h0T_(n):
                pe.wait_ge(a_h0, n.nth(HALVES, HALVES))
                if n.first:
                    pe.wait_ge(ld_head, 16)
                elif n.second:
                    pe.wait_ge(sel_done, 3)
                else:
                    pe.wait_ge(v_gx, n.before(K2))
                for k in range(K2):
                    for t in range(TILES):
                        last = tr(col_bank(n, k)[:, tile_of(t)], h0[:, t, tile_of(k)], ident)
                    last.then_inc(mm_h0T, 1)

            def x1T_(n):
                if n.first:
                    pe.wait_ge(comb_done, 1)
                for m in range(K2):
                    for k in range(K2):
                        if m == 0:
                            pe.wait_ge(a_hhi, n.nth(K2, k + 1))
                        mm(row_bank(n, m)[:, :], comb_hi[:, k, tile_of(m)], hT_hi[:, k, :], start=(k == 0), stop=False)
                        mm(row_bank(n, m)[:, :], comb_lo[:, k, tile_of(m)], hT_hi[:, k, :], start=False, stop=False)
                        if m == 0:
                            pe.wait_ge(v_hlo, n.nth(K2, k + 1))
                        last = mm(row_bank(n, m)[:, :], comb_hi[:, k, tile_of(m)], hT_lo[:, k, :], start=False,
                                  stop=(k == K2 - 1))
                    last.then_inc(mm_x1T, 1)

            def x1_(n):
                pe.wait_ge(g_x1T, n.nth(K2, K2))
                if n.second:
                    pe.wait_ge(v_gx, K2)
                for half in range(HALVES):
                    for t in (2 * half, 2 * half + 1):
                        for k in range(K2):
                            last = tr(pf[2 + half][:, (t % 2) * D + k * P:(t % 2) * D + (k + 1) * P],
                                      x1T[:, k, tile_of(t)], ident)
                    last.then_inc(mm_x1, 1)

            def aT_(n):
                if n.second:
                    pe.wait_ge(v_z, HALVES)
                pe.wait_ge(w_ready, n.nth(TILES, TILES))
                for t in range(TILES):
                    for k in range(K2):
                        for j in range(PAIR):
                            b = PAIR * t + j
                            last = mm(pf[0][j * HID:(j + 1) * HID, t * S:(t + 1) * S], w1_sb[:, b, k * HID:(k + 1) * HID],
                                      x1T[:, k, b * S:(b + 1) * S], start=(k == 0), stop=(k == K2 - 1))
                last.then_inc(mm_aT, 1)

            def z_(n):
                pe.wait_ge(g_ohl, n.nth(1, 1))
                if n.first:
                    pe.wait_ge(b2_done, 1)
                if n.second:
                    pe.wait_ge(v_sh, 1)
                pe.wait_ge(v_aT, n.nth(1, 1))
                pe.wait_ge(a_aT, n.nth(1, 1))
                for half in range(HALVES):
                    for t in (2 * half, 2 * half + 1):
                        bank = pf[1 - half][:, (t % 2) * D:(t % 2 + 1) * D]
                        mm(bank, flat(oh_lang[n.p][:, PAIR * t:PAIR * (t + 1), :]), b2_tab[:, :], start=True, stop=False)
                        last = mm(bank, aT[:, t, :], w2_sb[:, t, :], start=False, stop=True)
                    last.then_inc(mm_z, 1)

            def xnT_(n):
                if n.second:
                    pe.wait_ge(a_x1, 2 * HALVES)
                pe.wait_ge(v_zn, n.nth(TILES, TILES))
                for k in range(K2):
                    for t in range(TILES):
                        last = tr(pf[2 + k][:, tile_of(t)], zn[:, t, tile_of(k)], ident)
                    last.then_inc(mm_xnT, 1)

            def logits(n):
                pe.wait_ge(g_xnT, n.nth(1, 1))
                pe.wait_ge(v_xnT, n.nth(1, 1))
                for k in range(K2):
                    for t in range(TILES):
                        last = mm(pf[1][32 * t:32 * (t + 1), 0:P], rw[:, k, :], xnT[:, k, tile_of(t)],
                                  start=(k == 0), stop=(k == K2 - 1), tile_position=(0, 32 * t))
                last.then_inc(mm_lgT, 1)

            def route(n):
                pe.wait_ge(a_lgT, n.nth(1, 1))
                tr(pf[1][:, P:2 * P], lgT[:, :], ident).then_inc(mm_lg, 1)

            def y(n, c):
                t, q = c // 4, c % 4
                if c == 0:
                    pe.wait_ge(a_xhi, n.nth(K2, K2))
                    pe.wait_ge(v_xlo, n.nth(K2, K2))
                if n.first and c < EBANKS:
                    pe.wait_ge(we_done[q], 1)
                else:
                    pe.wait_ge(v_y, n.nth(E * TILES, 2 * (c - EBANKS + 1)))
                bank = pe_bank[c % EBANKS]
                for k in range(K2):
                    hi, lo = xn_hi[n.p][:, k, tile_of(t)], xn_lo[n.p][:, k, tile_of(t)]
                    mm(bank[:, :], hi, we_hi[:, q, k, :], start=(k == 0), stop=False)
                    mm(bank[:, :], hi, we_lo[:, q, k, :], start=False, stop=False)
                    last = mm(bank[:, :], lo, we_hi[:, q, k, :], start=False, stop=(k == K2 - 1))
                last.then_inc(mm_y, 1)

            run(pe, {"select": select, "combine1": combine1, "combine2": combine2, "h0": h0_, "h0T": h0T_,
                     "x1T": x1T_, "x1": x1_, "aT": aT_, "z": z_, "xnT": xnT_, "logits": logits,
                     "route": route, "y": y})

        @block.scalar
        def _(act):
            fn = nc.scalar.activation

            def prepare(n):
                act.wait_ge(warm_set, 1)
                fn(warm[:, :], warm[:, :], ACT.Tanh)

            def aT_(n):
                if n.first:
                    act.wait_ge(aT_zeroed, 1)
                    act.wait_ge(sel_done, 3)
                else:
                    act.wait_ge(mm_z, n.before(HALVES))
                act.wait_ge(mm_aT, n.nth(1, 1))
                for t in range(TILES):
                    last = fn(aT[HID:P, t, S:P], pf[0][HID:P, t * S:(t + 1) * S], ACT.Relu,
                              bias=b1T[HID:P, bass.ds(n.g * TILES + t, 1)])
                last.then_inc(a_aT, 1)

            def split_we(n, q):
                act.wait_ge(ld_we[q], 16 * K2)
                fn(flat(we_hi[:, q, :, :]), flat(we_in[:, q, :, :]), ACT.Copy).then_inc(we_hi_done[q], 1)

            def h0_(n, half):
                if half == 0 and not n.first:
                    act.wait_ge(mm_h0T, n.before(K2))
                act.wait_ge(mm_h0, n.nth(HALVES, half + 1))
                fn(flat(h0[:, 2 * half:2 * half + 2, :]), row_bank(n, half)[:, :], ACT.Copy).then_inc(a_h0, 1)

            def h0T_(n):
                if not n.first:
                    act.wait_ge(mm_x1T, n.before(K2))
                for k in range(K2):
                    act.wait_ge(mm_h0T, n.nth(K2, k + 1))
                    fn(hT_hi[:, k, :], col_bank(n, k)[:, :], ACT.Copy).then_inc(a_hhi, 1)

            def x1T_(n):
                if n.first:
                    act.wait_ge(ld_tail, 16)
                else:
                    act.wait_ge(g_x1T, n.before(K2))
                for m in range(K2):
                    act.wait_ge(mm_x1T, n.nth(K2, m + 1))
                    fn(th[:, m, :], row_bank(n, m)[:, :], ACT.Tanh, bias=bias_col[:, m:m + 1]).then_inc(a_th, 1)

            def x1_(n):
                if not n.early:
                    act.wait_ge(stored[n.p], n.i * 16 * TILES)
                for half in range(HALVES):
                    act.wait_ge(mm_x1, n.nth(HALVES, half + 1))
                    fn(flat(x1[n.p][:, 2 * half:2 * half + 2, :]), pf[2 + half][:, :], ACT.Copy).then_inc(a_x1, 1)

            def split_xn(n):
                if not n.early:
                    act.wait_ge(mm_y, n.before(CHUNKS, 2))
                act.wait_ge(g_xnT, n.nth(1, 1))
                fn(xn_hi[n.p][:, 0, :], xnT[:, 0, :], ACT.Copy).then_inc(a_xhi, 1)
                act.wait_ge(v_xnT, n.nth(1, 1))
                fn(xn_hi[n.p][:, 1, :], xnT[:, 1, :], ACT.Copy).then_inc(a_xhi, 1)

            def logits(n):
                if not n.first:
                    act.wait_ge(mm_lg, n.before(1))
                act.wait_ge(mm_lgT, n.nth(1, 1))
                fn(lgT[:, :], pf[1][:, 0:P], ACT.Identity, bias=rb_col).then_inc(a_lgT, 1)

            def route(n):
                act.wait_ge(v_sh, n.nth(1, 1))
                fn(ex[:, :, :], sh[:, :, :], ACT.Exp).then_inc(a_exp, 1)

            def store(n, t):
                act.wait_ge(v_y, n.nth(E * TILES, E * (t + 1)))
                act.dma_start(out[bass.ds(n.g * GT + t * P, P), :], x1[n.p][:, t, :]).then_inc(stored[n.p], 16)

            def store_last(n):
                store(Group(n.i, 0) if n.p == 1 else Group(n.i - 1, 1), TILES - 1)

            run(act, {"prepare": prepare, "adapter": lambda n, t: adapter(act, lambda o, i: fn(o, i, ACT.Copy), n, t, t == 0),
                      "aT": aT_, "split_we": split_we, "h0": h0_, "h0T": h0T_, "x1T": x1T_,
                      "x1": x1_, "split_xn": split_xn, "logits": logits, "route": route,
                      "store": store, "store_last": store_last})
            store(Group(GROUPS // 2 - 1, 1), TILES - 1)
            for p in range(2):
                act.wait_ge(stored[p], GROUPS // 2 * TILES * 16)

        @block.gpsimd
        def _(pool):
            tt = nc.gpsimd.tensor_tensor

            def prepare(n):
                nc.gpsimd.memset(warm[:, :], 0.0).then_inc(warm_set, 1)
                nc.gpsimd.memset(minus_half[:, :], -0.5).then_inc(zeroed, 1)
                nc.gpsimd.memset(is_cat[:, B:], 0.0).then_inc(zeroed, 1)
                nc.gpsimd.memset(is_lang[:, B:], 0.0).then_inc(zeroed, 1)
                nc.gpsimd.memset(aT[:, :, :], 0.0).then_inc(aT_zeroed, 1)

            def spread(src, n):
                return src[:, bass.ds(n.g * GB, GB)].unsqueeze(2).broadcast_to([P, GB, S])

            def onehots(n):
                if n.first:
                    pool.wait_ge(oh_small, 2)
                    pool.wait_ge(zeroed, 3)
                if not n.early:
                    pool.wait_ge(mm_h0, n.before(HALVES, 2))
                nc.gpsimd.tensor_copy(oh_cat[n.p][:, :, :], spread(is_cat, n)).then_inc(g_ohc, 1)
                if not n.early:
                    pool.wait_ge(mm_z, n.before(HALVES, 2))
                nc.gpsimd.tensor_copy(oh_lang[n.p][:, :, :], spread(is_lang, n)).then_inc(g_ohl, 1)

            def x1T_(n):
                pool.wait_ge(ld_a[n.p], n.loads(A_LOADS))
                if not n.first:
                    pool.wait_ge(mm_aT, n.before(1))
                for m in range(K2):
                    pool.wait_ge(a_th, n.nth(K2, m + 1))
                    tt(x1T[:, m, :], th[:, m, :], xT_sb[n.p][:, m, :], ALU.add).then_inc(g_x1T, 1)

            def z_(n):
                if not n.first:
                    pool.wait_ge(v_zn, n.before(TILES))
                pool.wait_ge(v_var, n.nth(1, 1))
                tt(rstd[:, :], var_eps, minus_half[:, :], ALU.pow).then_inc(g_rstd, 1)

            def split_we(n, q):
                if q in (1, 2):
                    pool.wait_ge(we_hi_done[q], 1)
                    tt(flat(we_lo[:, q, :, :]), flat(we_in[:, q, :, :]), flat(we_hi[:, q, :, :]).bitcast(F32),
                       ALU.subtract).then_inc(we_done[q], 1)

            def xnT_(n):
                if n.first:
                    pool.wait_ge(sel_done, 3)
                else:
                    pool.wait_ge(mm_lgT, n.before(1))
                    pool.wait_ge(a_xhi, n.before(K2))
                    pool.wait_ge(v_xlo, n.before(K2))
                pool.wait_ge(v_gx, n.nth(K2, 1))
                tt(by_batch(xnT[:, 0, :]), by_batch(gx[:, 0, :]), spread(betaT[:, 0, :], n), ALU.add
                   ).then_inc(g_xnT, 1)

            run(pool, {"prepare": prepare, "onehots": onehots, "x1T": x1T_, "split_we": split_we, "z": z_,
                       "xnT": xnT_})

        @block.vector
        def _(dve):
            tt, ts, stt, red = (nc.vector.tensor_tensor, nc.vector.tensor_scalar,
                                nc.vector.scalar_tensor_tensor, nc.vector.tensor_reduce)

            def split_table(dst, src, hi, done):
                nc.vector.tensor_copy(dst[:, :], src).then_inc(hi, 1)
                dve.wait_ge(hi, 1)
                tt(dst[NCAT:P, :], src[NCAT:P, :], dst[NCAT:P, :].bitcast(F32), ALU.subtract).then_inc(done, 1)

            def prepare(n):
                dve.wait_ge(ld_ids, 16)
                dve.wait_ge(ld_head, 16)
                ts(is_cat[:, 0:B], ids_in[:, 0, :], rowmod, None, ALU.is_equal).then_inc(oh_small, 1)
                ts(is_lang[:, 0:B], ids_in[:, 1, :], rowmod, None, ALU.is_equal).then_inc(oh_small, 1)
                split_table(bcat, bcat_in, bcat_hi, bcat_done)

            def combine1(n):
                dve.wait_ge(m1_mm, 1)
                nc.vector.tensor_copy(flat(m1T[:, :, :]), pe_bank[1][:, :]).then_inc(m1_done, 1)

            def combine2(n):
                dve.wait_ge(comb_mm, 1)
                nc.vector.tensor_copy(flat(comb_hi[:, :, :]), pe_bank[2][:, :]).then_inc(comb_hi_done, 1)
                dve.wait_ge(comb_hi_done, 1)
                tt(flat(comb_lo[:, :, :]), pe_bank[2][:, :], flat(comb_hi[:, :, :]).bitcast(F32), ALU.subtract
                   ).then_inc(comb_done, 1)

            def select(n):
                dve.wait_ge(ld_tail, 16)
                split_table(b2_tab, b2_in, b2_hi, b2_done)
                dve.wait_ge(sel_mm, 1)
                nc.vector.tensor_copy(flat(gammaT[:, :, :]), pe_bank[3][:, 0:2 * B]).then_inc(sel_done, 1)
                nc.vector.tensor_copy(flat(betaT[:, :, :]), pe_bank[3][:, 2 * B:4 * B]).then_inc(sel_done, 1)
                nc.vector.tensor_copy(b1T[:, :], pe_bank[3][:, 4 * B:4 * B + B // PAIR]).then_inc(sel_done, 1)

            def split_we(n, q):
                if q in (1, 2):
                    return
                dve.wait_ge(we_hi_done[q], 1)
                tt(flat(we_lo[:, q, :, :]), flat(we_in[:, q, :, :]), flat(we_hi[:, q, :, :]).bitcast(F32),
                   ALU.subtract).then_inc(we_done[q], 1)

            def h0T_(n):
                for k in range(K2):
                    dve.wait_ge(a_hhi, n.nth(K2, k + 1))
                    tt(hT_lo[:, k, :], col_bank(n, k)[:, :], hT_hi[:, k, :].bitcast(F32), ALU.subtract
                       ).then_inc(v_hlo, 1)

            def aT_(n):
                if n.first:
                    dve.wait_ge(aT_zeroed, 1)
                    dve.wait_ge(sel_done, 3)
                else:
                    dve.wait_ge(mm_z, n.before(HALVES))
                dve.wait_ge(mm_aT, n.nth(1, 1))
                for t in range(TILES):
                    last = ts(aT[0:HID, t, 0:S], pf[0][0:HID, t * S:(t + 1) * S],
                              b1T[0:HID, bass.ds(n.g * TILES + t, 1)], 0.0, ALU.add, ALU.max)
                last.then_inc(v_aT, 1)

            def z_(n):
                for half in range(HALVES):
                    dve.wait_ge(a_x1, n.nth(HALVES, half + 1))
                    dve.wait_ge(mm_z, n.nth(HALVES, half + 1))
                    tiles = slice(2 * half, 2 * half + 2)
                    tt(flat(z[:, tiles, :]), pf[1 - half][:, :], flat(x1[n.p][:, tiles, :]), ALU.add
                       ).then_inc(v_z, 1)
                    dve.wait_ge(v_z, n.nth(HALVES, half + 1))
                    for t in (2 * half, 2 * half + 1):
                        nc.vector.bn_stats(stats[:, t, :], z[:, t, :]).then_inc(v_stats, 1)
                mean_e, mean_o, m2_e, m2_o = (stats[:, :, c] for c in (1, 4, 2, 5))
                dve.wait_ge(v_stats, n.nth(TILES, TILES))
                tt(moments[:, 0, :], mean_e, mean_o, ALU.add).then_inc(v_mom, 1)
                tt(moments[:, 1, :], mean_e, mean_o, ALU.subtract).then_inc(v_mom, 1)
                tt(moments[:, 2, :], m2_e, m2_o, ALU.add).then_inc(v_mom, 1)
                dve.wait_ge(v_mom, n.nth(6, 3))
                stt(moments[:, 3, :], moments[:, 1, :], 0.25, moments[:, 1, :], ALU.mult, ALU.mult
                    ).then_inc(v_mom, 1)
                ts(moments[:, 4, :], moments[:, 2, :], 1.0 / D, LN_EPS, ALU.mult, ALU.add).then_inc(v_mom, 1)
                ts(mean, moments[:, 0, :], 0.5, None, ALU.mult).then_inc(v_mom, 1)
                dve.wait_ge(v_mom, n.nth(6, 6))
                tt(var_eps, moments[:, 3, :], moments[:, 4, :], ALU.add).then_inc(v_var, 1)

            def zn_(n):
                if not n.first:
                    dve.wait_ge(mm_xnT, n.before(K2))
                dve.wait_ge(g_rstd, n.nth(1, 1))
                for t in range(TILES):
                    ts(zn[:, t, :], z[:, t, :], mean[:, t:t + 1], rstd[:, t:t + 1], ALU.subtract, ALU.mult
                       ).then_inc(v_zn, 1)

            def xnT_(n):
                if not n.first:
                    dve.wait_ge(g_xnT, n.before(1))
                for k in range(K2):
                    dve.wait_ge(mm_xnT, n.nth(K2, k + 1))
                    tt(by_batch(gx[:, k, :]), by_batch(pf[2 + k][:, :]), spread(gammaT[:, k, :], n), ALU.mult
                       ).then_inc(v_gx, 1)
                if not n.first:
                    dve.wait_ge(mm_lgT, n.before(1))
                    dve.wait_ge(a_xhi, n.before(K2))
                dve.wait_ge(v_gx, n.nth(K2, K2))
                tt(by_batch(xnT[:, 1, :]), by_batch(gx[:, 1, :]), spread(betaT[:, 1, :], n), ALU.add
                   ).then_inc(v_xnT, 1)

            def spread(src, n):
                return src[:, bass.ds(n.g * GB, GB)].unsqueeze(2).broadcast_to([P, GB, S])

            def split_xn(n):
                for k in range(K2):
                    dve.wait_ge(a_xhi, n.nth(K2, k + 1))
                    tt(xn_lo[n.p][:, k, :], xnT[:, k, :], xn_hi[n.p][:, k, :].bitcast(F32), ALU.subtract
                       ).then_inc(v_xlo, 1)

            STEPS = 20

            def route(n):
                top, k1, second, k2, total, both, den, r_den, w_sum, clipped, scale, factor = (
                    small[:, i, :] for i in range(12))
                step = [0]

                def seq(ins):
                    step[0] += 1
                    ins.then_inc(v_seq, 1)
                    dve.wait_ge(v_seq, n.nth(STEPS, step[0]))

                def wide(column):
                    return column.unsqueeze(2).broadcast_to([P, TILES, E])

                lg = pf[1][:, P:2 * P].rearrange("p (t c) -> p t c", t=TILES)[:, :, 0:E]
                dve.wait_ge(mm_lg, n.nth(1, 1))
                seq(red(top, lg, AX, ALU.max))
                tt(sh[:, :, :], lg, wide(top), ALU.subtract).then_inc(v_sh, 1)
                dve.wait_ge(v_sh, n.nth(1, 1))
                seq(stt(key1[:, :, :], sh[:, :, :], 0.0, rank_sb[:, :, :], ALU.is_equal, ALU.mult))
                seq(red(k1, key1[:, :, :], AX, ALU.max))
                seq(tt(oh1[:, :, :], key1[:, :, :], wide(k1), ALU.is_equal))
                seq(stt(sh2[:, :, :], oh1[:, :, :], -BIG, sh[:, :, :], ALU.mult, ALU.add))
                seq(red(second, sh2[:, :, :], AX, ALU.max))
                seq(tt(key2[:, :, :], sh2[:, :, :], wide(second), ALU.is_equal))
                seq(tt(key2[:, :, :], key2[:, :, :], rank_sb[:, :, :], ALU.mult))
                seq(red(k2, key2[:, :, :], AX, ALU.max))
                seq(tt(oh2[:, :, :], key2[:, :, :], wide(k2), ALU.is_equal))
                dve.wait_ge(a_exp, n.nth(1, 1))
                red(total, ex[:, :, :], AX, ALU.add).then_inc(v_total, 1)
                seq(tt(oh2[:, :, :], oh2[:, :, :], oh1[:, :, :], ALU.add))
                seq(tt(pr[:, :, :], ex[:, :, :], oh2[:, :, :], ALU.mult))
                seq(red(both, pr[:, :, :], AX, ALU.add))
                dve.wait_ge(v_total, n.nth(1, 1))
                seq(stt(den, total, EPS, both, ALU.mult, ALU.add))
                seq(nc.vector.reciprocal(r_den, den))
                seq(tt(w_sum, both, r_den, ALU.mult))
                ts(scale, w_sum, EPS, 1.0, ALU.mult, ALU.add).then_inc(v_scale, 1)
                seq(ts(clipped, w_sum, EPS, None, ALU.max))
                seq(nc.vector.reciprocal(factor, clipped))
                dve.wait_ge(v_scale, n.nth(1, 1))
                seq(tt(factor, factor, scale, ALU.mult))
                seq(tt(factor, factor, r_den, ALU.mult))
                tt(gate[n.p][:, :, :], pr[:, :, :], wide(factor), ALU.mult).then_inc(v_gate, 1)
                assert step[0] == STEPS, step

            def add(n, c):
                t, q = c // 4, c % 4
                if c == 0:
                    dve.wait_ge(v_gate, n.nth(1, 1))
                dve.wait_ge(mm_y, n.nth(CHUNKS, c + 1))
                for h in range(2):
                    e = 2 * q + h
                    if e > 0:
                        dve.wait_ge(v_y, n.nth(E * TILES, c * 2 + h))
                    stt(x1[n.p][:, t, :], pe_bank[c % EBANKS][:, h * D:(h + 1) * D], gate[n.p][:, t, e:e + 1],
                        x1[n.p][:, t, :], ALU.mult, ALU.add).then_inc(v_y, 1)

            run(dve, {"prepare": prepare, "combine1": combine1, "combine2": combine2, "select": select,
                      "adapter_v": lambda n, t: adapter(dve, nc.vector.tensor_copy, n, t, t == 2),
                      "split_we": split_we, "h0T": h0T_, "aT": aT_, "z": z_, "zn": zn_, "xnT": xnT_,
                      "split_xn": split_xn, "route": route, "add": add})


def kernel(x, itok_B_0_63, itok_B_0_8, L0_cond_W, L0_cond_b, L0_ffn_weight, L0_ffn_aux_weight1,
           L0_ffn_aux_weight2, L0_ffn_bias, L1_cond_W1, L1_cond_b1, L1_cond_W2, L1_cond_b2,
           L1_cond_gamma, L1_cond_beta, L1_ffn_router_w, L1_ffn_router_b, L1_ffn_expert_weights):
    import numpy as np
    import concourse.bacc as bacc
    from concourse.bass_utils import run_bass_kernel_spmd

    def lay(a):
        return np.ascontiguousarray(a)

    def by_chunk(w):
        return np.concatenate([w[k * P:(k + 1) * P] for k in range(K2)], axis=1)

    head = np.concatenate([np.eye(P, dtype=np.float32), (np.arange(P) % NCAT).astype(np.float32).reshape(P, 1),
                           np.tile(np.arange(E, 0, -1).astype(np.float32), (P, TILES)),
                           np.tile(np.asarray(L0_cond_b), (2, 1))], axis=1)
    tail = np.zeros((P, TAIL), np.float32)
    tail[:NLANG, :3 * D + HID] = np.concatenate([np.asarray(a) for a in (
        L1_cond_gamma, L1_cond_beta, L1_cond_b1, L1_cond_b2)], axis=1)
    tail[NCAT:NCAT + NLANG, 2 * D + HID:3 * D + HID] = L1_cond_b2
    tail[:, 3 * D + HID:3 * D + HID + K2] = np.asarray(L0_ffn_bias).reshape(K2, P).T
    for t in range(TILES):
        tail[32 * t:32 * t + E, TAIL - K2 * 32 - 1] = L1_ffn_router_b
    for k in range(K2):
        at = TAIL - K2 * 32 + k * 32
        tail[:, at:at + E] = np.asarray(L1_ffn_router_w)[:, k * P:(k + 1) * P].T
    ids = np.concatenate([np.asarray(itok_B_0_63), np.asarray(itok_B_0_8)])
    arrays = {
        "xT": lay(np.asarray(x).reshape(TOK, D).T),
        "ids": lay(np.broadcast_to(ids, (P, 2 * B))),
        "head": lay(head),
        "L0W": lay(L0_cond_W),
        "L0_mats": lay(np.concatenate([by_chunk(np.asarray(L0_ffn_weight).T), by_chunk(np.asarray(L0_ffn_aux_weight1)),
                                       by_chunk(np.asarray(L0_ffn_aux_weight2))], axis=1)),
        "tail": tail,
        "W1": lay(np.asarray(L1_cond_W1).reshape(NLANG, K2, P, HID).transpose(0, 2, 1, 3)
                  .reshape(NLANG, P, K2 * HID)),
        "W2": lay(L1_cond_W2),
        "We": lay(L1_ffn_expert_weights),
    }
    nc = bacc.Bacc("TRN2", target_bir_lowering=False, num_devices=1)
    args = {name: nc.dram_tensor(name, a.shape, mybir.dt.from_np(a.dtype), kind="ExternalInput").ap()
            for name, a in arrays.items()}
    args["out"] = nc.dram_tensor("out", (TOK, D), F32, kind="ExternalOutput").ap()
    build(nc, **args)
    r = run_bass_kernel_spmd(nc, [arrays], core_ids=[0])
    return r.results[0]["out"].reshape(B, S, D)
```

```python
from contextlib import ExitStack

import concourse.bass as bass
from concourse import mybir

ALU = mybir.AluOpType
ACT = mybir.ActivationFunctionType
AX = mybir.AxisListType.X
F32 = mybir.dt.float32
F32R = mybir.dt.float32r
I32 = mybir.dt.int32

P = 128
B = 64
S = 64
D = 256
K2 = D // P
HID = 64
NCAT = 64
NLANG = 10
E = 8
TOK = B * S
PAIR = 2
TILES = 4
GB = TILES * PAIR
GT = TILES * P
GROUPS = TOK // GT
CHUNKS = TILES * E // 2
EBANKS = 4
HALVES = 2
HEAD = P + 1 + TILES * E + D
TAIL = 3 * D + HID + K2 + 1 + K2 * 32
LN_EPS = 1e-5
EPS = 1e-10
BIG = 3.0e38


class Group:

    def __init__(self, i, p, early=False):
        self.i, self.p, self.g = i, p, 2 * i + p
        self.early, self.first = early, early and self.g == 0
        self.second = early and self.g == 1

    def nth(self, per_group, n):
        return self.g * per_group + n

    def before(self, per_group, back=1):
        return (self.g - back + 1) * per_group

    def loads(self, per_group):
        return (self.i + 1) * per_group


def start_up():
    a, b, c = Group(0, 0, early=True), Group(0, 1, early=True), Group(1, 0)
    yield from (
        ("prepare", a), ("onehots", a), ("onehots", b), ("combine1", a), ("h0", a, 0), ("combine2", a),
        ("h0", a, 1), ("select", a), ("h0T", a), ("adapter_dve", a, 2), ("adapter_dve", a, 3), ("adapter", a, 0))
    yield from (
        ("x1T", a), ("adapter", a, 1), ("x1", a), ("aT", a), ("split_we", a, 0), ("h0", b, 0), ("z", a),
        ("split_we", a, 1), ("adapter", b, 0), ("h0", b, 1), ("h0T", b), ("zn", a), ("adapter", b, 1),
        ("x1T", b), ("xnT", a), ("split_we", a, 2), ("split_we", a, 3), ("split_xn", a), ("logits", a),
        ("x1", b), ("adapter", b, 2), ("route", a), ("adapter", b, 3))
    yield from experts(a, {
        (0, 0): (("onehots", c),), (3, 0): (("aT", b),), (5, 0): (("z", b),), (9, 0): (("zn", b),),
        (11, 0): (("xnT", b),), (14, 0): (("split_xn", b),)}, behind=2)
    yield ("logits", b)


def turn(e, f, after):
    yield from experts(e, {
        (0, 0): (("h0", f, 0), ("route", e),), (1, 0): (("adapter", f, 0),), (2, 0): (("h0", f, 1),),
        (3, 0): (("adapter", f, 1), ("h0T", f), ("adapter", f, 3),), (4, 1): (("x1T", f),),
        (6, 1): (("adapter", f, 2),), (7, 0): (("x1", f), ("aT", f),), (8, 0): (("z", f),),
        (10, 0): (("onehots", after),), (10, 1): (("zn", f),), (13, 1): (("xnT", f),),
        (14, 0): (("split_xn", f),)})
    yield ("logits", f)


def last_turn(e):
    yield from experts(e, {(0, 0): (("route", e),)})


def experts(e, front, behind=0):
    for c in range(CHUNKS + behind):
        yield from front.get((c, 0), ())
        if c < CHUNKS:
            yield ("y", e, c)
        yield from front.get((c, 1), ())
        if c >= behind:
            yield ("add", e, c - behind)
            done = c - behind - 2
            if done % 4 == 3 and 0 < done < CHUNKS - 4:
                yield ("store", e, done // 4)
        if c == 1 and not e.first:
            yield ("store_last", e)


def build(nc, xT, ids, head, L0W, L0_mats, tail, W1, W2, We, out):
    with ExitStack() as ctx:
        def sb(name, shape, dt=F32):
            return ctx.enter_context(nc.sbuf_tensor(name, shape, dt))

        def sem(name):
            return ctx.enter_context(nc.semaphore(name))

        head_in = sb("head_in", [P, HEAD])
        ident, rowmod = head_in[:, 0:P], head_in[:, P:P + 1]
        rank_sb = head_in[:, P + 1:P + 1 + TILES * E].rearrange("p (t e) -> p t e", t=TILES)
        bcat_in = head_in[:, HEAD - D:HEAD]
        tail_in = sb("tail_in", [P, TAIL])
        lang_in, b2_in = tail_in[0:NLANG, 0:2 * D + HID], tail_in[:, 2 * D + HID:3 * D + HID]
        bias_col = tail_in[:, 3 * D + HID:3 * D + HID + K2]
        rb_col = tail_in[:, TAIL - K2 * 32 - 1:TAIL - K2 * 32]
        rw = tail_in[:, TAIL - K2 * 32:TAIL].rearrange("p (k e) -> p k e", k=K2)
        ids_in = sb("ids_in", [P, 2, B], I32)
        is_cat = sb("is_cat", [P, B + GB])
        is_lang = sb("is_lang", [P, B + GB])
        bcat = sb("bcat", [P, D], F32R)
        b2_tab = sb("b2_tab", [P, D], F32R)
        gammaT = sb("gammaT", [P, K2, B])
        betaT = sb("betaT", [P, K2, B])
        b1T = sb("b1T", [P, B // PAIR])
        mats = sb("mats", [P, 3, K2, D])
        m1T = sb("m1T", [P, K2, D])
        comb_hi = sb("comb_hi", [P, K2, D], F32R)
        comb_lo = sb("comb_lo", [P, K2, D], F32R)
        w1_tab = sb("w1_tab", [P, NLANG, K2 * HID])
        w2_tab = sb("w2_tab", [HID, NLANG, D])
        we_in = sb("we_in", [P, E // 2, K2, 2 * D])
        we_hi = sb("we_hi", [P, E // 2, K2, 2 * D], F32R)
        we_lo = sb("we_lo", [P, E // 2, K2, 2 * D], F32R)
        minus_half = sb("minus_half", [P, TILES])
        warm = sb("warm", [P, 1])

        w_cat = [sb(f"w_cat{p}", [P, GB, K2, D]) for p in range(2)]
        xT_sb = [sb(f"xT_sb{p}", [P, K2, GT]) for p in range(2)]
        w1_sb = sb("w1_sb", [P, GB, K2 * HID])
        w2_sb = sb("w2_sb", [P, TILES, D])
        oh_cat = [sb(f"oh_cat{p}", [P, GB, S], F32R) for p in range(2)]
        oh_lang = [sb(f"oh_lang{p}", [P, GB, S], F32R) for p in range(2)]
        h0 = sb("h0", [P, TILES, D])
        hT_hi = sb("hT_hi", [P, K2, GT], F32R)
        hT_lo = sb("hT_lo", [P, K2, GT], F32R)
        th = sb("th", [P, K2, GT])
        x1T = sb("x1T", [P, K2, GT])
        x1 = [sb(f"x1_{p}", [P, TILES, D]) for p in range(2)]
        aT = sb("aT", [P, TILES, P])
        z = sb("z", [P, TILES, D])
        stats = sb("stats", [P, TILES, 6])
        moments = sb("moments", [P, 7, TILES])
        mean, var_eps = moments[:, 5, :], moments[:, 6, :]
        rstd = sb("rstd", [P, TILES])
        zn = sb("zn", [P, TILES, D])
        gx = sb("gx", [P, K2, GT])
        xnT = sb("xnT", [P, K2, GT])
        xn_hi = [sb(f"xn_hi{p}", [P, K2, GT], F32R) for p in range(2)]
        xn_lo = [sb(f"xn_lo{p}", [P, K2, GT], F32R) for p in range(2)]
        lgT = sb("lgT", [P, P])
        sh = sb("sh", [P, TILES, E])
        ex = sb("ex", [P, TILES, E])
        key1 = sb("key1", [P, TILES, E])
        oh1 = sb("oh1", [P, TILES, E])
        sh2 = sb("sh2", [P, TILES, E])
        key2 = sb("key2", [P, TILES, E])
        oh2 = sb("oh2", [P, TILES, E])
        pr = sb("pr", [P, TILES, E])
        small = sb("small", [P, 12, TILES])
        gate = [sb(f"gate{p}", [P, TILES, E]) for p in range(2)]

        pf = [ctx.enter_context(nc.psum_tensor(f"pf{i}", [P, 512], F32)) for i in range(4)]
        pe_bank = [ctx.enter_context(nc.psum_tensor(f"pe{i}", [P, 512], F32)) for i in range(EBANKS)]

        ld_ids, ld_head, ld_mats, ld_tail, ld_tabs = (
            sem(n) for n in ("ld_ids", "ld_head", "ld_mats", "ld_tail", "ld_tabs"))
        ld_a = [sem(f"ld_a{p}") for p in range(2)]
        ld_b = [sem(f"ld_b{p}") for p in range(2)]
        ld_we = [sem(f"ld_we{q}") for q in range(E // 2)]
        stored = [sem(f"stored{p}") for p in range(2)]
        consts_set, oh_small, bcat_hi, bcat_done, b2_hi, b2_done = (
            sem(n) for n in ("consts_set", "oh_small", "bcat_hi", "bcat_done", "b2_hi", "b2_done"))
        sel_mm, sel_done, m1_mm, m1_done, comb_mm, comb_hi_done, comb_done = (
            sem(n) for n in ("sel_mm", "sel_done", "m1_mm", "m1_done", "comb_mm", "comb_hi_done", "comb_done"))
        we_hi_done = [sem(f"we_hi_done{q}") for q in range(E // 2)]
        we_done = [sem(f"we_done{q}") for q in range(E // 2)]
        mm_h0, mm_h0T, mm_x1T, mm_x1, mm_aT, mm_z, mm_xnT, mm_lgT, mm_lg, mm_y = (
            sem(n) for n in ("mm_h0", "mm_h0T", "mm_x1T", "mm_x1", "mm_aT", "mm_z", "mm_xnT", "mm_lgT",
                             "mm_lg", "mm_y"))
        act_h0, act_hhi, w_ready, act_th, act_aT, act_x1, act_lgT, act_xhi, act_exp = (
            sem(n) for n in ("act_h0", "act_hhi", "w_ready", "act_th", "act_aT", "act_x1", "act_lgT", "act_xhi",
                             "act_exp"))
        warm_set, aT_zeroed, dve_stats, dve_mom, dve_var, dve_xnT, dve_total, dve_scale = (
            sem(n) for n in ("warm_set", "aT_zeroed", "dve_stats", "dve_mom", "dve_var", "dve_xnT", "dve_total",
                             "dve_scale"))
        dve_hlo, dve_aT, dve_z, dve_zn, dve_gx, dve_xlo, dve_sh, dve_gate, dve_y, dve_seq = (
            sem(n) for n in ("dve_hlo", "dve_aT", "dve_z", "dve_zn", "dve_gx", "dve_xlo", "dve_sh",
                             "dve_gate", "dve_y", "dve_seq"))
        pool_ohc, pool_ohl, x1T_done, pool_rstd, pool_xnT = (
            sem(n) for n in ("pool_ohc", "pool_ohl", "x1T_done", "pool_rstd", "pool_xnT"))

        A_LOADS, B_LOADS = 16 * (1 + GB // 2), 16 * (GB // 2)
        block = ctx.enter_context(nc.Block())

        def row_bank(n, i):
            return pe_bank[i] if n.second else pf[i]

        def col_bank(n, k):
            return pe_bank[2 + k] if n.second else pf[2 + k]

        def tile_of(t):
            return slice(t * P, (t + 1) * P)

        def flat(ap):
            return ap.rearrange("p a n -> p (a n)")

        def by_batch(ap):
            return ap.rearrange("p (b s) -> p b s", s=S)

        def run(eng, stages):
            def walk(items):
                for name, n, *more in items:
                    if name in stages:
                        stages[name](n, *more)

            walk(start_up())
            with eng.Fori(0, (GROUPS - 2) // 2) as i:
                walk(turn(Group(i, 1), Group(i + 1, 0), Group(i + 1, 1)))
                walk(turn(Group(i + 1, 0), Group(i + 1, 1), Group(i + 2, 0)))
            walk(last_turn(Group(GROUPS // 2 - 1, 1)))

        @block.sync
        def _(sp):
            def load_x(n):
                sp.dma_start(xT_sb[n.p][:, :, :],
                             xT[:, bass.ds(n.g * GT, GT)].rearrange("(k p) t -> p k t", p=P)
                             ).then_inc(ld_a[n.p], 16)

            def load_cat(n):
                for b in range(GB):
                    cat = sp.value_load(ids_in[0:1, 0, bass.ds(n.g * GB + b, 1)], min_val=0, max_val=NCAT - 1)
                    sp.dma_start(w_cat[n.p][:, b, :, :],
                                 L0W[bass.ds(cat, 1), :, :].rearrange("o (k p) n -> p (o k) n", p=P)
                                 ).then_inc(ld_a[n.p] if b < GB // 2 else ld_b[n.p], 16)

            a, b = Group(0, 0, early=True), Group(0, 1, early=True)
            sp.dma_start(ids_in[:, :, :], ids.rearrange("p (a b) -> p a b", a=2)).then_inc(ld_ids, 16)
            sp.dma_start(head_in[:, :], head).then_inc(ld_head, 16)
            sp.dma_start(mats[:, :, :, :].rearrange("p m k n -> p (m k n)"), L0_mats).then_inc(ld_mats, 16)
            load_x(a)
            sp.wait_ge(ld_ids, 16)
            load_cat(a)
            sp.dma_start(tail_in[:, :], tail).then_inc(ld_tail, 16)
            sp.dma_start(w1_tab[:, :, :], W1.rearrange("l p n -> p l n")).then_inc(ld_tabs, 16)
            sp.dma_start(w2_tab[:, :, :], W2.rearrange("l a n -> a l n")).then_inc(ld_tabs, 16)
            load_x(b)
            load_cat(b)
            for q in range(E // 2):
                for k in range(K2):
                    sp.dma_start(we_in[:, q, k, :].rearrange("p (e n) -> p e n", n=D),
                                 We[2 * q:2 * q + 2, k * P:(k + 1) * P, :].rearrange("e p n -> p e n")
                                 ).then_inc(ld_we[q], 16)
            with sp.Fori(1, GROUPS // 2) as i:
                for p in range(2):
                    n = Group(i, p)
                    sp.wait_ge(mm_h0, n.before(HALVES, 2))
                    sp.wait_ge(x1T_done, n.before(K2, 2))
                    load_x(n)
                    load_cat(n)

        @block.tensor
        def _(pe):
            mm, tr = nc.tensor.matmul, nc.tensor.transpose

            def select(n):
                pe.wait_ge(ld_tail, 16)
                for m in range(2 * K2):
                    mm(pe_bank[3][:, m * B:(m + 1) * B], lang_in[:, m * P:(m + 1) * P], is_lang[0:NLANG, 0:B],
                       start=True, stop=True)
                for j in range(PAIR):
                    last = mm(pe_bank[3][j * HID:(j + 1) * HID, 4 * B:4 * B + B // PAIR],
                              lang_in[:, 2 * D:2 * D + HID], is_lang[0:NLANG, j:B:PAIR], start=True, stop=True)
                last.then_inc(sel_mm, 1)

            def combine1(n):
                pe.wait_ge(ld_mats, 16)
                for m in range(K2):
                    for k in range(K2):
                        last = mm(pe_bank[1][:, m * D:(m + 1) * D], mats[:, 1, k, tile_of(m)], mats[:, 0, k, :],
                                  start=(k == 0), stop=(k == K2 - 1))
                last.then_inc(m1_mm, 1)

            def combine2(n):
                pe.wait_ge(m1_done, 1)
                for m in range(K2):
                    for k in range(K2):
                        last = mm(pe_bank[2][:, m * D:(m + 1) * D], m1T[:, k, tile_of(m)], mats[:, 2, k, :],
                                  start=(k == 0), stop=(k == K2 - 1))
                last.then_inc(comb_mm, 1)

            def h0_(n, half):
                if half == 0:
                    pe.wait_ge(pool_ohc, n.nth(1, 1))
                    if n.first:
                        pe.wait_ge(bcat_done, 1)
                    elif not n.second:
                        pe.wait_ge(dve_z, n.before(HALVES))
                    pe.wait_ge(ld_a[n.p], n.loads(A_LOADS))
                else:
                    if not n.early:
                        pe.wait_ge(dve_sh, n.before(1))
                    pe.wait_ge(ld_b[n.p], n.loads(B_LOADS))
                for t in (2 * half, 2 * half + 1):
                    bank = row_bank(n, half)[:, (t % 2) * D:(t % 2 + 1) * D]
                    mm(bank, flat(oh_cat[n.p][:, PAIR * t:PAIR * (t + 1), :]), bcat[:, :], start=True, stop=False,
                       skip_group_check=True)
                    for k in range(K2):
                        for j in range(PAIR):
                            b = PAIR * t + j
                            last = mm(bank[j * S:(j + 1) * S, :], xT_sb[n.p][:, k, b * S:(b + 1) * S],
                                      w_cat[n.p][:, b, k, :], start=False, stop=(k == K2 - 1),
                                      skip_group_check=True)
                last.then_inc(mm_h0, 1)

            def h0T_(n):
                pe.wait_ge(act_h0, n.nth(HALVES, HALVES))
                if n.first:
                    pe.wait_ge(ld_head, 16)
                elif n.second:
                    pe.wait_ge(sel_done, 3)
                else:
                    pe.wait_ge(dve_gx, n.before(K2))
                for k in range(K2):
                    for t in range(TILES):
                        last = tr(col_bank(n, k)[:, tile_of(t)], h0[:, t, tile_of(k)], ident)
                    last.then_inc(mm_h0T, 1)

            def x1T_(n):
                if n.first:
                    pe.wait_ge(comb_done, 1)
                for m in range(K2):
                    for k in range(K2):
                        if m == 0:
                            pe.wait_ge(act_hhi, n.nth(K2, k + 1))
                        mm(row_bank(n, m)[:, :], comb_hi[:, k, tile_of(m)], hT_hi[:, k, :], start=(k == 0), stop=False)
                        mm(row_bank(n, m)[:, :], comb_lo[:, k, tile_of(m)], hT_hi[:, k, :], start=False, stop=False)
                        if m == 0:
                            pe.wait_ge(dve_hlo, n.nth(K2, k + 1))
                        last = mm(row_bank(n, m)[:, :], comb_hi[:, k, tile_of(m)], hT_lo[:, k, :], start=False,
                                  stop=(k == K2 - 1))
                    last.then_inc(mm_x1T, 1)

            def x1_(n):
                pe.wait_ge(x1T_done, n.nth(K2, K2))
                if n.second:
                    pe.wait_ge(dve_gx, K2)
                for half in range(HALVES):
                    for t in (2 * half, 2 * half + 1):
                        for k in range(K2):
                            last = tr(pf[2 + half][:, (t % 2) * D + k * P:(t % 2) * D + (k + 1) * P],
                                      x1T[:, k, tile_of(t)], ident)
                    last.then_inc(mm_x1, 1)

            def aT_(n):
                if n.second:
                    pe.wait_ge(dve_z, HALVES)
                pe.wait_ge(w_ready, n.nth(TILES, TILES))
                for t in range(TILES):
                    for k in range(K2):
                        for j in range(PAIR):
                            b = PAIR * t + j
                            last = mm(pf[0][j * HID:(j + 1) * HID, t * S:(t + 1) * S],
                                      w1_sb[:, b, k * HID:(k + 1) * HID],
                                      x1T[:, k, b * S:(b + 1) * S], start=(k == 0), stop=(k == K2 - 1))
                last.then_inc(mm_aT, 1)

            def z_(n):
                pe.wait_ge(pool_ohl, n.nth(1, 1))
                if n.first:
                    pe.wait_ge(b2_done, 1)
                if n.second:
                    pe.wait_ge(dve_sh, 1)
                pe.wait_ge(dve_aT, n.nth(1, 1))
                pe.wait_ge(act_aT, n.nth(1, 1))
                for half in range(HALVES):
                    for t in (2 * half, 2 * half + 1):
                        bank = pf[1 - half][:, (t % 2) * D:(t % 2 + 1) * D]
                        mm(bank, flat(oh_lang[n.p][:, PAIR * t:PAIR * (t + 1), :]), b2_tab[:, :], start=True, stop=False)
                        last = mm(bank, aT[:, t, :], w2_sb[:, t, :], start=False, stop=True)
                    last.then_inc(mm_z, 1)

            def xnT_(n):
                if n.second:
                    pe.wait_ge(act_x1, 2 * HALVES)
                pe.wait_ge(dve_zn, n.nth(TILES, TILES))
                for k in range(K2):
                    for t in range(TILES):
                        last = tr(pf[2 + k][:, tile_of(t)], zn[:, t, tile_of(k)], ident)
                    last.then_inc(mm_xnT, 1)

            def logits(n):
                pe.wait_ge(pool_xnT, n.nth(1, 1))
                pe.wait_ge(dve_xnT, n.nth(1, 1))
                for k in range(K2):
                    for t in range(TILES):
                        last = mm(pf[1][32 * t:32 * (t + 1), 0:P], rw[:, k, :], xnT[:, k, tile_of(t)],
                                  start=(k == 0), stop=(k == K2 - 1), tile_position=(0, 32 * t))
                last.then_inc(mm_lgT, 1)

            def route(n):
                pe.wait_ge(act_lgT, n.nth(1, 1))
                tr(pf[1][:, P:2 * P], lgT[:, :], ident).then_inc(mm_lg, 1)

            def y(n, c):
                t, q = c // 4, c % 4
                if c == 0:
                    pe.wait_ge(act_xhi, n.nth(K2, K2))
                    pe.wait_ge(dve_xlo, n.nth(K2, K2))
                if n.first and c < EBANKS:
                    pe.wait_ge(we_done[q], 1)
                else:
                    pe.wait_ge(dve_y, n.nth(E * TILES, 2 * (c - EBANKS + 1)))
                bank = pe_bank[c % EBANKS]
                for k in range(K2):
                    hi, lo = xn_hi[n.p][:, k, tile_of(t)], xn_lo[n.p][:, k, tile_of(t)]
                    mm(bank[:, :], hi, we_hi[:, q, k, :], start=(k == 0), stop=False)
                    mm(bank[:, :], hi, we_lo[:, q, k, :], start=False, stop=False)
                    last = mm(bank[:, :], lo, we_hi[:, q, k, :], start=False, stop=(k == K2 - 1))
                last.then_inc(mm_y, 1)

            run(pe, {"select": select, "combine1": combine1, "combine2": combine2, "h0": h0_, "h0T": h0T_,
                     "x1T": x1T_, "x1": x1_, "aT": aT_, "z": z_, "xnT": xnT_, "logits": logits,
                     "route": route, "y": y})

        @block.scalar
        def _(act):
            fn = nc.scalar.activation

            def prepare(n):
                act.wait_ge(warm_set, 1)
                fn(warm[:, :], warm[:, :], ACT.Tanh)

            def adapter(n, t):
                for j in range(PAIR):
                    b = PAIR * t + j
                    lang = act.value_load(ids_in[0:1, 1, bass.ds(n.g * GB + b, 1)], min_val=0, max_val=NLANG - 1)
                    if n.first:
                        act.wait_ge(ld_tabs, 16 * 2)
                    elif b == 0:
                        act.wait_ge(mm_z, n.before(HALVES))
                    fn(w1_sb[:, b, :], w1_tab[:, bass.ds(lang, 1), :].rearrange("p l n -> p (l n)"), ACT.Copy)
                    last = fn(w2_sb[j * HID:(j + 1) * HID, t, :],
                              w2_tab[:, bass.ds(lang, 1), :].rearrange("p l n -> p (l n)"), ACT.Copy)
                last.then_inc(w_ready, 1)

            def aT_(n):
                if n.first:
                    act.wait_ge(aT_zeroed, 1)
                    act.wait_ge(sel_done, 3)
                else:
                    act.wait_ge(mm_z, n.before(HALVES))
                act.wait_ge(mm_aT, n.nth(1, 1))
                for t in range(TILES):
                    last = fn(aT[HID:P, t, S:P], pf[0][HID:P, t * S:(t + 1) * S], ACT.Relu,
                              bias=b1T[HID:P, bass.ds(n.g * TILES + t, 1)])
                last.then_inc(act_aT, 1)

            def split_we(n, q):
                act.wait_ge(ld_we[q], 16 * K2)
                fn(flat(we_hi[:, q, :, :]), flat(we_in[:, q, :, :]), ACT.Copy).then_inc(we_hi_done[q], 1)

            def h0_(n, half):
                if half == 0 and not n.first:
                    act.wait_ge(mm_h0T, n.before(K2))
                act.wait_ge(mm_h0, n.nth(HALVES, half + 1))
                fn(flat(h0[:, 2 * half:2 * half + 2, :]), row_bank(n, half)[:, :], ACT.Copy).then_inc(act_h0, 1)

            def h0T_(n):
                if not n.first:
                    act.wait_ge(mm_x1T, n.before(K2))
                for k in range(K2):
                    act.wait_ge(mm_h0T, n.nth(K2, k + 1))
                    fn(hT_hi[:, k, :], col_bank(n, k)[:, :], ACT.Copy).then_inc(act_hhi, 1)

            def x1T_(n):
                if n.first:
                    act.wait_ge(ld_tail, 16)
                else:
                    act.wait_ge(x1T_done, n.before(K2))
                for m in range(K2):
                    act.wait_ge(mm_x1T, n.nth(K2, m + 1))
                    fn(th[:, m, :], row_bank(n, m)[:, :], ACT.Tanh, bias=bias_col[:, m:m + 1]).then_inc(act_th, 1)

            def x1_(n):
                if not n.early:
                    act.wait_ge(stored[n.p], n.i * 16 * TILES)
                for half in range(HALVES):
                    act.wait_ge(mm_x1, n.nth(HALVES, half + 1))
                    fn(flat(x1[n.p][:, 2 * half:2 * half + 2, :]), pf[2 + half][:, :], ACT.Copy).then_inc(act_x1, 1)

            def split_xn(n):
                if not n.early:
                    act.wait_ge(mm_y, n.before(CHUNKS, 2))
                act.wait_ge(pool_xnT, n.nth(1, 1))
                fn(xn_hi[n.p][:, 0, :], xnT[:, 0, :], ACT.Copy).then_inc(act_xhi, 1)
                act.wait_ge(dve_xnT, n.nth(1, 1))
                fn(xn_hi[n.p][:, 1, :], xnT[:, 1, :], ACT.Copy).then_inc(act_xhi, 1)

            def logits(n):
                if not n.first:
                    act.wait_ge(mm_lg, n.before(1))
                act.wait_ge(mm_lgT, n.nth(1, 1))
                fn(lgT[:, :], pf[1][:, 0:P], ACT.Identity, bias=rb_col).then_inc(act_lgT, 1)

            def route(n):
                act.wait_ge(dve_sh, n.nth(1, 1))
                fn(ex[:, :, :], sh[:, :, :], ACT.Exp).then_inc(act_exp, 1)

            def store(n, t):
                act.wait_ge(dve_y, n.nth(E * TILES, E * (t + 1)))
                act.dma_start(out[bass.ds(n.g * GT + t * P, P), :], x1[n.p][:, t, :]).then_inc(stored[n.p], 16)

            def store_last(n):
                store(Group(n.i, 0) if n.p == 1 else Group(n.i - 1, 1), TILES - 1)

            run(act, {"prepare": prepare, "adapter": adapter, "aT": aT_, "split_we": split_we, "h0": h0_,
                      "h0T": h0T_, "x1T": x1T_,
                      "x1": x1_, "split_xn": split_xn, "logits": logits, "route": route,
                      "store": store, "store_last": store_last})
            store(Group(GROUPS // 2 - 1, 1), TILES - 1)
            for p in range(2):
                act.wait_ge(stored[p], GROUPS // 2 * TILES * 16)

        @block.gpsimd
        def _(pool):
            tt = nc.gpsimd.tensor_tensor

            def prepare(n):
                nc.gpsimd.memset(warm[:, :], 0.0).then_inc(warm_set, 1)
                nc.gpsimd.memset(minus_half[:, :], -0.5).then_inc(consts_set, 1)
                nc.gpsimd.memset(is_cat[:, B:], 0.0).then_inc(consts_set, 1)
                nc.gpsimd.memset(is_lang[:, B:], 0.0).then_inc(consts_set, 1)
                nc.gpsimd.memset(aT[:, :, :], 0.0).then_inc(aT_zeroed, 1)

            def spread(src, n):
                return src[:, bass.ds(n.g * GB, GB)].unsqueeze(2).broadcast_to([P, GB, S])

            def onehots(n):
                if n.first:
                    pool.wait_ge(oh_small, 2)
                    pool.wait_ge(consts_set, 3)
                if not n.early:
                    pool.wait_ge(mm_h0, n.before(HALVES, 2))
                nc.gpsimd.tensor_copy(oh_cat[n.p][:, :, :], spread(is_cat, n)).then_inc(pool_ohc, 1)
                if not n.early:
                    pool.wait_ge(mm_z, n.before(HALVES, 2))
                nc.gpsimd.tensor_copy(oh_lang[n.p][:, :, :], spread(is_lang, n)).then_inc(pool_ohl, 1)

            def x1T_(n):
                pool.wait_ge(ld_a[n.p], n.loads(A_LOADS))
                if not n.first:
                    pool.wait_ge(mm_aT, n.before(1))
                for m in range(1 if n.first else K2):
                    pool.wait_ge(act_th, n.nth(K2, m + 1))
                    tt(x1T[:, m, :], th[:, m, :], xT_sb[n.p][:, m, :], ALU.add).then_inc(x1T_done, 1)

            def z_(n):
                if not n.first:
                    pool.wait_ge(dve_zn, n.before(TILES))
                pool.wait_ge(dve_var, n.nth(1, 1))
                tt(rstd[:, :], var_eps, minus_half[:, :], ALU.pow).then_inc(pool_rstd, 1)

            def split_we(n, q):
                if q in (1, 2):
                    pool.wait_ge(we_hi_done[q], 1)
                    tt(flat(we_lo[:, q, :, :]), flat(we_in[:, q, :, :]), flat(we_hi[:, q, :, :]).bitcast(F32),
                       ALU.subtract).then_inc(we_done[q], 1)

            def xnT_(n):
                if n.first:
                    pool.wait_ge(sel_done, 3)
                else:
                    pool.wait_ge(mm_lgT, n.before(1))
                    pool.wait_ge(act_xhi, n.before(K2))
                    pool.wait_ge(dve_xlo, n.before(K2))
                pool.wait_ge(dve_gx, n.nth(K2, 1))
                tt(by_batch(xnT[:, 0, :]), by_batch(gx[:, 0, :]), spread(betaT[:, 0, :], n), ALU.add
                   ).then_inc(pool_xnT, 1)

            run(pool, {"prepare": prepare, "onehots": onehots, "x1T": x1T_, "split_we": split_we, "z": z_,
                       "xnT": xnT_})

        @block.vector
        def _(dve):
            tt, ts, stt, red = (nc.vector.tensor_tensor, nc.vector.tensor_scalar,
                                nc.vector.scalar_tensor_tensor, nc.vector.tensor_reduce)
            copy = nc.vector.tensor_copy

            def split_table(dst, src, hi, done):
                copy(dst[:, :], src).then_inc(hi, 1)
                dve.wait_ge(hi, 1)
                tt(dst[NCAT:P, :], src[NCAT:P, :], dst[NCAT:P, :].bitcast(F32), ALU.subtract).then_inc(done, 1)

            def prepare(n):
                dve.wait_ge(ld_ids, 16)
                dve.wait_ge(ld_head, 16)
                ts(is_cat[:, 0:B], ids_in[:, 0, :], rowmod, None, ALU.is_equal).then_inc(oh_small, 1)
                ts(is_lang[:, 0:B], ids_in[:, 1, :], rowmod, None, ALU.is_equal).then_inc(oh_small, 1)
                split_table(bcat, bcat_in, bcat_hi, bcat_done)

            def combine1(n):
                dve.wait_ge(m1_mm, 1)
                copy(flat(m1T[:, :, :]), pe_bank[1][:, :]).then_inc(m1_done, 1)

            def combine2(n):
                dve.wait_ge(comb_mm, 1)
                copy(flat(comb_hi[:, :, :]), pe_bank[2][:, :]).then_inc(comb_hi_done, 1)
                dve.wait_ge(comb_hi_done, 1)
                tt(flat(comb_lo[:, :, :]), pe_bank[2][:, :], flat(comb_hi[:, :, :]).bitcast(F32), ALU.subtract
                   ).then_inc(comb_done, 1)

            def select(n):
                dve.wait_ge(ld_tail, 16)
                split_table(b2_tab, b2_in, b2_hi, b2_done)
                dve.wait_ge(sel_mm, 1)
                copy(flat(gammaT[:, :, :]), pe_bank[3][:, 0:2 * B]).then_inc(sel_done, 1)
                copy(flat(betaT[:, :, :]), pe_bank[3][:, 2 * B:4 * B]).then_inc(sel_done, 1)
                copy(b1T[:, :], pe_bank[3][:, 4 * B:4 * B + B // PAIR]).then_inc(sel_done, 1)

            def split_we(n, q):
                if q in (1, 2):
                    return
                dve.wait_ge(we_hi_done[q], 1)
                tt(flat(we_lo[:, q, :, :]), flat(we_in[:, q, :, :]), flat(we_hi[:, q, :, :]).bitcast(F32),
                   ALU.subtract).then_inc(we_done[q], 1)

            def h0T_(n):
                for k in range(K2):
                    dve.wait_ge(act_hhi, n.nth(K2, k + 1))
                    tt(hT_lo[:, k, :], col_bank(n, k)[:, :], hT_hi[:, k, :].bitcast(F32), ALU.subtract
                       ).then_inc(dve_hlo, 1)

            def adapter(n, t):
                for j in range(PAIR):
                    b = PAIR * t + j
                    lang = dve.value_load(ids_in[0:1, 1, bass.ds(n.g * GB + b, 1)], min_val=0, max_val=NLANG - 1)
                    dve.wait_ge(ld_tabs, 16 * 2)
                    copy(w1_sb[:, b, :], w1_tab[:, bass.ds(lang, 1), :].rearrange("p l n -> p (l n)"))
                    last = copy(w2_sb[j * HID:(j + 1) * HID, t, :],
                                w2_tab[:, bass.ds(lang, 1), :].rearrange("p l n -> p (l n)"))
                last.then_inc(w_ready, 1)

            def x1T_(n):
                if n.first:
                    dve.wait_ge(ld_a[0], A_LOADS)
                    dve.wait_ge(act_th, K2)
                    tt(x1T[:, 1, :], th[:, 1, :], xT_sb[0][:, 1, :], ALU.add).then_inc(x1T_done, 1)

            def aT_(n):
                if n.first:
                    dve.wait_ge(aT_zeroed, 1)
                    dve.wait_ge(sel_done, 3)
                else:
                    dve.wait_ge(mm_z, n.before(HALVES))
                dve.wait_ge(mm_aT, n.nth(1, 1))
                for t in range(TILES):
                    last = ts(aT[0:HID, t, 0:S], pf[0][0:HID, t * S:(t + 1) * S],
                              b1T[0:HID, bass.ds(n.g * TILES + t, 1)], 0.0, ALU.add, ALU.max)
                last.then_inc(dve_aT, 1)

            def z_(n):
                for half in range(HALVES):
                    dve.wait_ge(act_x1, n.nth(HALVES, half + 1))
                    dve.wait_ge(mm_z, n.nth(HALVES, half + 1))
                    tiles = slice(2 * half, 2 * half + 2)
                    tt(flat(z[:, tiles, :]), pf[1 - half][:, :], flat(x1[n.p][:, tiles, :]), ALU.add
                       ).then_inc(dve_z, 1)
                    dve.wait_ge(dve_z, n.nth(HALVES, half + 1))
                    for t in (2 * half, 2 * half + 1):
                        nc.vector.bn_stats(stats[:, t, :], z[:, t, :]).then_inc(dve_stats, 1)
                mean_e, mean_o, m2_e, m2_o = (stats[:, :, c] for c in (1, 4, 2, 5))
                dve.wait_ge(dve_stats, n.nth(TILES, TILES))
                tt(moments[:, 0, :], mean_e, mean_o, ALU.add).then_inc(dve_mom, 1)
                tt(moments[:, 1, :], mean_e, mean_o, ALU.subtract).then_inc(dve_mom, 1)
                tt(moments[:, 2, :], m2_e, m2_o, ALU.add).then_inc(dve_mom, 1)
                dve.wait_ge(dve_mom, n.nth(6, 3))
                stt(moments[:, 3, :], moments[:, 1, :], 0.25, moments[:, 1, :], ALU.mult, ALU.mult
                    ).then_inc(dve_mom, 1)
                ts(moments[:, 4, :], moments[:, 2, :], 1.0 / D, LN_EPS, ALU.mult, ALU.add).then_inc(dve_mom, 1)
                ts(mean, moments[:, 0, :], 0.5, None, ALU.mult).then_inc(dve_mom, 1)
                dve.wait_ge(dve_mom, n.nth(6, 6))
                tt(var_eps, moments[:, 3, :], moments[:, 4, :], ALU.add).then_inc(dve_var, 1)

            def zn_(n):
                if not n.first:
                    dve.wait_ge(mm_xnT, n.before(K2))
                dve.wait_ge(pool_rstd, n.nth(1, 1))
                for t in range(TILES):
                    ts(zn[:, t, :], z[:, t, :], mean[:, t:t + 1], rstd[:, t:t + 1], ALU.subtract, ALU.mult
                       ).then_inc(dve_zn, 1)

            def xnT_(n):
                if not n.first:
                    dve.wait_ge(pool_xnT, n.before(1))
                for k in range(K2):
                    dve.wait_ge(mm_xnT, n.nth(K2, k + 1))
                    tt(by_batch(gx[:, k, :]), by_batch(pf[2 + k][:, :]), spread(gammaT[:, k, :], n), ALU.mult
                       ).then_inc(dve_gx, 1)
                if not n.first:
                    dve.wait_ge(mm_lgT, n.before(1))
                    dve.wait_ge(act_xhi, n.before(K2))
                dve.wait_ge(dve_gx, n.nth(K2, K2))
                tt(by_batch(xnT[:, 1, :]), by_batch(gx[:, 1, :]), spread(betaT[:, 1, :], n), ALU.add
                   ).then_inc(dve_xnT, 1)

            def spread(src, n):
                return src[:, bass.ds(n.g * GB, GB)].unsqueeze(2).broadcast_to([P, GB, S])

            def split_xn(n):
                for k in range(K2):
                    dve.wait_ge(act_xhi, n.nth(K2, k + 1))
                    tt(xn_lo[n.p][:, k, :], xnT[:, k, :], xn_hi[n.p][:, k, :].bitcast(F32), ALU.subtract
                       ).then_inc(dve_xlo, 1)

            STEPS = 20

            def route(n):
                top, k1, second, k2, total, both, den, r_den, w_sum, clipped, scale, factor = (
                    small[:, i, :] for i in range(12))
                step = [0]

                def seq(ins):
                    step[0] += 1
                    ins.then_inc(dve_seq, 1)
                    dve.wait_ge(dve_seq, n.nth(STEPS, step[0]))

                def wide(column):
                    return column.unsqueeze(2).broadcast_to([P, TILES, E])

                lg = pf[1][:, P:2 * P].rearrange("p (t c) -> p t c", t=TILES)[:, :, 0:E]
                dve.wait_ge(mm_lg, n.nth(1, 1))
                seq(red(top, lg, AX, ALU.max))
                tt(sh[:, :, :], lg, wide(top), ALU.subtract).then_inc(dve_sh, 1)
                dve.wait_ge(dve_sh, n.nth(1, 1))
                seq(stt(key1[:, :, :], sh[:, :, :], 0.0, rank_sb[:, :, :], ALU.is_equal, ALU.mult))
                seq(red(k1, key1[:, :, :], AX, ALU.max))
                seq(tt(oh1[:, :, :], key1[:, :, :], wide(k1), ALU.is_equal))
                seq(stt(sh2[:, :, :], oh1[:, :, :], -BIG, sh[:, :, :], ALU.mult, ALU.add))
                seq(red(second, sh2[:, :, :], AX, ALU.max))
                seq(tt(key2[:, :, :], sh2[:, :, :], wide(second), ALU.is_equal))
                seq(tt(key2[:, :, :], key2[:, :, :], rank_sb[:, :, :], ALU.mult))
                seq(red(k2, key2[:, :, :], AX, ALU.max))
                seq(tt(oh2[:, :, :], key2[:, :, :], wide(k2), ALU.is_equal))
                dve.wait_ge(act_exp, n.nth(1, 1))
                red(total, ex[:, :, :], AX, ALU.add).then_inc(dve_total, 1)
                seq(tt(oh2[:, :, :], oh2[:, :, :], oh1[:, :, :], ALU.add))
                seq(tt(pr[:, :, :], ex[:, :, :], oh2[:, :, :], ALU.mult))
                seq(red(both, pr[:, :, :], AX, ALU.add))
                dve.wait_ge(dve_total, n.nth(1, 1))
                seq(stt(den, total, EPS, both, ALU.mult, ALU.add))
                seq(nc.vector.reciprocal(r_den, den))
                seq(tt(w_sum, both, r_den, ALU.mult))
                ts(scale, w_sum, EPS, 1.0, ALU.mult, ALU.add).then_inc(dve_scale, 1)
                seq(ts(clipped, w_sum, EPS, None, ALU.max))
                seq(nc.vector.reciprocal(factor, clipped))
                dve.wait_ge(dve_scale, n.nth(1, 1))
                seq(tt(factor, factor, scale, ALU.mult))
                seq(tt(factor, factor, r_den, ALU.mult))
                tt(gate[n.p][:, :, :], pr[:, :, :], wide(factor), ALU.mult).then_inc(dve_gate, 1)
                assert step[0] == STEPS, step

            def add(n, c):
                t, q = c // 4, c % 4
                if c == 0:
                    dve.wait_ge(dve_gate, n.nth(1, 1))
                dve.wait_ge(mm_y, n.nth(CHUNKS, c + 1))
                for h in range(2):
                    e = 2 * q + h
                    if e > 0:
                        dve.wait_ge(dve_y, n.nth(E * TILES, c * 2 + h))
                    stt(x1[n.p][:, t, :], pe_bank[c % EBANKS][:, h * D:(h + 1) * D], gate[n.p][:, t, e:e + 1],
                        x1[n.p][:, t, :], ALU.mult, ALU.add).then_inc(dve_y, 1)

            run(dve, {"prepare": prepare, "combine1": combine1, "combine2": combine2, "select": select,
                      "adapter_dve": adapter,
                      "split_we": split_we, "h0T": h0T_, "x1T": x1T_, "aT": aT_, "z": z_, "zn": zn_, "xnT": xnT_,
                      "split_xn": split_xn, "route": route, "add": add})


def kernel(x, itok_B_0_63, itok_B_0_8, L0_cond_W, L0_cond_b, L0_ffn_weight, L0_ffn_aux_weight1,
           L0_ffn_aux_weight2, L0_ffn_bias, L1_cond_W1, L1_cond_b1, L1_cond_W2, L1_cond_b2,
           L1_cond_gamma, L1_cond_beta, L1_ffn_router_w, L1_ffn_router_b, L1_ffn_expert_weights):
    import numpy as np
    import concourse.bacc as bacc
    from concourse.bass_utils import run_bass_kernel_spmd

    def lay(a):
        return np.ascontiguousarray(a)

    def by_chunk(w):
        return np.concatenate([w[k * P:(k + 1) * P] for k in range(K2)], axis=1)

    head = np.concatenate([np.eye(P, dtype=np.float32), (np.arange(P) % NCAT).astype(np.float32).reshape(P, 1),
                           np.tile(np.arange(E, 0, -1).astype(np.float32), (P, TILES)),
                           np.tile(np.asarray(L0_cond_b), (2, 1))], axis=1)
    tail = np.zeros((P, TAIL), np.float32)
    tail[:NLANG, :3 * D + HID] = np.concatenate([np.asarray(a) for a in (
        L1_cond_gamma, L1_cond_beta, L1_cond_b1, L1_cond_b2)], axis=1)
    tail[NCAT:NCAT + NLANG, 2 * D + HID:3 * D + HID] = L1_cond_b2
    tail[:, 3 * D + HID:3 * D + HID + K2] = np.asarray(L0_ffn_bias).reshape(K2, P).T
    for t in range(TILES):
        tail[32 * t:32 * t + E, TAIL - K2 * 32 - 1] = L1_ffn_router_b
    for k in range(K2):
        at = TAIL - K2 * 32 + k * 32
        tail[:, at:at + E] = np.asarray(L1_ffn_router_w)[:, k * P:(k + 1) * P].T
    ids = np.concatenate([np.asarray(itok_B_0_63), np.asarray(itok_B_0_8)])
    arrays = {
        "xT": lay(np.asarray(x).reshape(TOK, D).T),
        "ids": lay(np.broadcast_to(ids, (P, 2 * B))),
        "head": lay(head),
        "L0W": lay(L0_cond_W),
        "L0_mats": lay(np.concatenate([by_chunk(np.asarray(L0_ffn_weight).T), by_chunk(np.asarray(L0_ffn_aux_weight1)),
                                       by_chunk(np.asarray(L0_ffn_aux_weight2))], axis=1)),
        "tail": tail,
        "W1": lay(np.asarray(L1_cond_W1).reshape(NLANG, K2, P, HID).transpose(0, 2, 1, 3)
                  .reshape(NLANG, P, K2 * HID)),
        "W2": lay(L1_cond_W2),
        "We": lay(L1_ffn_expert_weights),
    }
    nc = bacc.Bacc("TRN2", target_bir_lowering=False, num_devices=1)
    args = {name: nc.dram_tensor(name, a.shape, mybir.dt.from_np(a.dtype), kind="ExternalInput").ap()
            for name, a in arrays.items()}
    args["out"] = nc.dram_tensor("out", (TOK, D), F32, kind="ExternalOutput").ap()
    build(nc, **args)
    r = run_bass_kernel_spmd(nc, [arrays], core_ids=[0])
    return r.results[0]["out"].reshape(B, S, D)
```
